# Optimizing a Trainium2 kernel written in Bass

```python
import numpy as np
import jax
import jax.numpy as jnp

def _softmax(x, axis=-1):
    return jax.nn.softmax(x, axis=axis)

def _gelu(x):
    return jax.nn.gelu(x, approximate=True)

def _silu(x):
    return jax.nn.silu(x)

def _sigmoid(x):
    return jax.nn.sigmoid(x)

def _layernorm(x, axis=-1, eps=1e-05):
    m = jnp.mean(x, axis=axis, keepdims=True)
    v = jnp.var(x, axis=axis, keepdims=True)
    return (x - m) / jnp.sqrt(v + eps)

def _scatter_add(tgt, idx, src, axis=0):
    return tgt.at[idx].add(src)

def _segment_sum(src, seg, n):
    return jax.ops.segment_sum(src, seg, n)
kernel_name = 'mk_xattn_ffn_d1_seqx_r4_727180'

def setup_inputs(seed: int=0):
    np.random.seed(seed)
    _w = jnp.asarray

    def _rec_inputs():
        import jax
        import jax.numpy as jnp
        _rk = jax.random.key(seed)
        x = 7.22e-05 + 1 * jax.random.normal(jax.random.fold_in(_rk, 1), (64, 256, 256), jnp.float32)
        _lenS = 256 - jax.random.randint(jax.random.fold_in(_rk, 7), (64,), 0, max(1, 256 // 4) + 1, jnp.int32)
        _lenS2 = 120 - jax.random.randint(jax.random.fold_in(_rk, 8), (64,), 0, max(1, 120 // 4) + 1, jnp.int32)
        _ctx_1024P = jax.random.normal(jax.random.fold_in(_rk, 11), (64, 16, 256), jnp.float32)
        _ctx_1024c = jax.random.dirichlet(jax.random.fold_in(_rk, 511), 0.3 * jnp.ones((16,), jnp.float32), (64, 120))
        _ctx_1024t = jnp.einsum('bsk,bkd->bsd', _ctx_1024c, _ctx_1024P)
        _ctx_1024t = _ctx_1024t * jax.lax.rsqrt(jnp.mean(jnp.square(_ctx_1024t)) + 1e-12) * 0.953939
        ctx_1024 = 4.13588e-05 + 0.999923 * (_ctx_1024t + 0.3 * jax.random.normal(jax.random.fold_in(_rk, 611), (64, 120, 256), jnp.float32))
        _validS = jnp.arange(256)[None, :] < _lenS[:, None]
        _validS2 = jnp.arange(120)[None, :] < _lenS2[:, None]
        _causal = jnp.tril(jnp.ones((256, 256), dtype=bool))
        mask_Bx1xS2_bk0 = jnp.logical_not(jnp.broadcast_to(_validS2[:, None, :], (64, 1, 120)))
        return (x, ctx_1024, mask_Bx1xS2_bk0)
    x, ctx_1024, mask_Bx1xS2_bk0 = _rec_inputs()

    def _L0_xattn_setup():
        import jax, jax.numpy as jnp
        import numpy as np
        B, S, E, H = (4, 512, 256, 16)
        DH = E // H

        def _make_heads(v, n_heads):
            b, n, e = v.shape
            return jnp.moveaxis(v.reshape(b, n, n_heads, e // n_heads), -2, 0)
        key = jax.random.key(seed)
        k1, k2, k3, k4, k5 = jax.random.split(key, 5)
        return {'query': jax.random.normal(k1, (B, S, E), dtype=jnp.float32), 'key': jax.random.normal(k2, (B, S, E), dtype=jnp.float32), 'value': jax.random.normal(k3, (B, S, E), dtype=jnp.float32), 'mask': jax.random.randint(k4, (B, 1, S), 0, 2).astype(bool), 'W_out': jax.random.normal(k5, (E, E), dtype=jnp.float32) / np.sqrt(E), 'scale': jnp.asarray(1.0, dtype=jnp.float32), 'log_C': jnp.asarray(np.log(10.0), dtype=jnp.float32)}
    _L0_xattn_all = _L0_xattn_setup()
    _L0_xattn_in = {k: v for k, v in _L0_xattn_all.items() if k in ('W_out', 'scale', 'log_C')}
    del _L0_xattn_all

    def _L0_ffn_setup():
        import jax, jax.numpy as jnp
        import numpy as np
        B, S, DIM = (4, 1024, 256)
        BASE_COUPLING = 0.1
        NUM_CYCLES = 3

        def _gelu(x):
            return jax.nn.gelu(x, approximate=False)

        def _coupling_net(h, w1, b1, w2, b2, w3, b3, w4, b4):
            h = _gelu(h @ w1 + b1)
            h = _gelu(h @ w2 + b2)
            h = _gelu(h @ w3 + b3)
            return jax.nn.sigmoid(h @ w4 + b4)

        def _global_net(h, w1, b1, w2, b2, w3, b3):
            h = _gelu(h @ w1 + b1)
            h = _gelu(h @ w2 + b2)
            return jax.nn.sigmoid(h @ w3 + b3)

        def _twist(x):
            o_r, o_i, p_r, p_i = jnp.split(x, 4, axis=-1)
            return jnp.concatenate([p_r, -p_i, -o_r, o_i], axis=-1)
        key = jax.random.key(seed)
        ks = jax.random.split(key, 9)
        d = DIM

        def w(k, fan_in, fan_out):
            return jax.random.normal(k, (fan_in, fan_out), dtype=jnp.float32) / np.sqrt(fan_in).astype(np.float32)
        inp = {'x': jax.random.normal(ks[0], (B, S, d), dtype=jnp.float32)}
        cn_dims = [(d, d), (d, d // 2), (d // 2, d // 4), (d // 4, 1)]
        for i, (a, b) in enumerate(cn_dims):
            inp[f'cn_w{i + 1}'] = w(ks[1 + i], a, b)
            inp[f'cn_b{i + 1}'] = jnp.zeros((b,), dtype=jnp.float32)
        gc_dims = [(d, d // 2), (d // 2, d // 4), (d // 4, 1)]
        for i, (a, b) in enumerate(gc_dims):
            inp[f'gc_w{i + 1}'] = w(ks[5 + i], a, b)
            inp[f'gc_b{i + 1}'] = jnp.zeros((b,), dtype=jnp.float32)
        inp['adaptive_range'] = jnp.full((1,), 0.2, dtype=jnp.float32)
        return inp
    _L0_ffn_all = _L0_ffn_setup()
    _L0_ffn_in = {k: v for k, v in _L0_ffn_all.items() if k in ('cn_w1', 'cn_b1', 'cn_w2', 'cn_b2', 'cn_w3', 'cn_b3', 'cn_w4', 'cn_b4', 'gc_w1', 'gc_b1', 'gc_w2', 'gc_b2', 'gc_w3', 'gc_b3', 'adaptive_range')}
    del _L0_ffn_all
    return {'x': x, 'ctx_1024': ctx_1024, 'mask_Bx1xS2_bk0': mask_Bx1xS2_bk0, 'L0_xattn_W_out': _L0_xattn_in['W_out'], 'L0_xattn_scale': _L0_xattn_in['scale'], 'L0_xattn_log_C': _L0_xattn_in['log_C'], 'L0_ffn_cn_w1': _L0_ffn_in['cn_w1'], 'L0_ffn_cn_b1': _L0_ffn_in['cn_b1'], 'L0_ffn_cn_w2': _L0_ffn_in['cn_w2'], 'L0_ffn_cn_b2': _L0_ffn_in['cn_b2'], 'L0_ffn_cn_w3': _L0_ffn_in['cn_w3'], 'L0_ffn_cn_b3': _L0_ffn_in['cn_b3'], 'L0_ffn_cn_w4': _L0_ffn_in['cn_w4'], 'L0_ffn_cn_b4': _L0_ffn_in['cn_b4'], 'L0_ffn_gc_w1': _L0_ffn_in['gc_w1'], 'L0_ffn_gc_b1': _L0_ffn_in['gc_b1'], 'L0_ffn_gc_w2': _L0_ffn_in['gc_w2'], 'L0_ffn_gc_b2': _L0_ffn_in['gc_b2'], 'L0_ffn_gc_w3': _L0_ffn_in['gc_w3'], 'L0_ffn_gc_b3': _L0_ffn_in['gc_b3'], 'L0_ffn_adaptive_range': _L0_ffn_in['adaptive_range']}

def reference(x, ctx_1024, mask_Bx1xS2_bk0, L0_xattn_W_out, L0_xattn_scale, L0_xattn_log_C, L0_ffn_cn_w1, L0_ffn_cn_b1, L0_ffn_cn_w2, L0_ffn_cn_b2, L0_ffn_cn_w3, L0_ffn_cn_b3, L0_ffn_cn_w4, L0_ffn_cn_b4, L0_ffn_gc_w1, L0_ffn_gc_b1, L0_ffn_gc_w2, L0_ffn_gc_b2, L0_ffn_gc_w3, L0_ffn_gc_b3, L0_ffn_adaptive_range):
    import jax
    import jax.numpy as jnp

    def _L0_xattn_ref(query, key, value, mask, W_out, scale, log_C):
        import jax, jax.numpy as jnp
        import numpy as np
        B, S, E, H = (4, 512, 256, 16)
        DH = E // H

        def _make_heads(v, n_heads):
            b, n, e = v.shape
            return jnp.moveaxis(v.reshape(b, n, n_heads, e // n_heads), -2, 0)
        q = _make_heads(query, H)
        k = _make_heads(key, H)
        v = _make_heads(value, H)
        d_k = q.shape[-1]
        u = jnp.einsum('hbqd,hbkd->hbqk', q, k) * scale / np.sqrt(d_k)
        logits = jnp.tanh(u) * jnp.exp(log_C)
        logits = jnp.where(mask, -jnp.inf, logits)
        attn = jax.nn.softmax(logits, axis=-1)
        out_heads = jnp.einsum('hbqk,hbkd->hbqd', attn, v)
        out = jnp.moveaxis(out_heads, 0, -2).reshape(query.shape)
        return out @ W_out.T

    def _L0_ffn_ref(x, cn_w1, cn_b1, cn_w2, cn_b2, cn_w3, cn_b3, cn_w4, cn_b4, gc_w1, gc_b1, gc_w2, gc_b2, gc_w3, gc_b3, adaptive_range):
        import jax, jax.numpy as jnp
        import numpy as np
        B, S, DIM = (4, 1024, 256)
        BASE_COUPLING = 0.1
        NUM_CYCLES = 3

        def _gelu(x):
            return jax.nn.gelu(x, approximate=False)

        def _coupling_net(h, w1, b1, w2, b2, w3, b3, w4, b4):
            h = _gelu(h @ w1 + b1)
            h = _gelu(h @ w2 + b2)
            h = _gelu(h @ w3 + b3)
            return jax.nn.sigmoid(h @ w4 + b4)

        def _global_net(h, w1, b1, w2, b2, w3, b3):
            h = _gelu(h @ w1 + b1)
            h = _gelu(h @ w2 + b2)
            return jax.nn.sigmoid(h @ w3 + b3)

        def _twist(x):
            o_r, o_i, p_r, p_i = jnp.split(x, 4, axis=-1)
            return jnp.concatenate([p_r, -p_i, -o_r, o_i], axis=-1)
        global_context = x.mean(axis=1, keepdims=True)
        gf = _global_net(global_context, gc_w1, gc_b1, gc_w2, gc_b2, gc_w3, gc_b3)
        out = x
        for _ in range(NUM_CYCLES):
            tf = _coupling_net(out, cn_w1, cn_b1, cn_w2, cn_b2, cn_w3, cn_b3, cn_w4, cn_b4)
            combined = 0.7 * gf + 0.3 * tf
            coupling = BASE_COUPLING + adaptive_range * (combined - 0.5) * 2.0
            out = out + coupling * _twist(out)
        return out
    x = x + _L0_xattn_ref(_layernorm(x, axis=-1), ctx_1024, ctx_1024, mask_Bx1xS2_bk0, L0_xattn_W_out, L0_xattn_scale, L0_xattn_log_C)
    x = x + _L0_ffn_ref(_layernorm(x, axis=-1), L0_ffn_cn_w1, L0_ffn_cn_b1, L0_ffn_cn_w2, L0_ffn_cn_b2, L0_ffn_cn_w3, L0_ffn_cn_b3, L0_ffn_cn_w4, L0_ffn_cn_b4, L0_ffn_gc_w1, L0_ffn_gc_b1, L0_ffn_gc_w2, L0_ffn_gc_b2, L0_ffn_gc_w3, L0_ffn_gc_b3, L0_ffn_adaptive_range)
    return x

_drawn_inputs = setup_inputs


def setup_inputs(seed=0):
    import zlib

    import numpy as np

    out = dict(_drawn_inputs(seed))
    spreads = {'L0_ffn_cn_b1': (0.0, 2.0),
     'L0_ffn_cn_b2': (0.0, 2.0),
     'L0_ffn_cn_b3': (0.0, 2.0),
     'L0_ffn_gc_b1': (0.0, 0.8),
     'L0_ffn_gc_b2': (0.0, 2.0)}
    factors = {'L0_ffn_cn_w1': 8.0,
     'L0_ffn_cn_w2': 8.0,
     'L0_ffn_cn_w3': 6.771,
     'L0_ffn_cn_w4': 7.833,
     'L0_ffn_gc_w1': 6.431,
     'L0_ffn_gc_w2': 6.558,
     'L0_ffn_gc_w3': 4.946}
    for name, (base, spread) in spreads.items():
        noise = np.random.default_rng([zlib.crc32(name.encode()), seed]).standard_normal(out[name].shape)
        drawn = base * np.exp(spread * noise) if base else spread * noise
        out[name] = jnp.asarray(drawn.astype(out[name].dtype))
    for name, factor in factors.items():
        out[name] = (out[name] * factor).astype(out[name].dtype)
    return out
```

```python
from contextlib import ExitStack

import concourse.bass as bass
from concourse import mybir

ALU = mybir.AluOpType
ACT = mybir.ActivationFunctionType
AX = mybir.AxisListType
F32 = mybir.dt.float32
F16 = mybir.dt.float16
U8 = mybir.dt.uint8

P = 128
EPS = 1e-5
MASKED = -1e30
EXP_ROOM = 64.0
Q_SCALE = 256.0
K_SCALE = 256.0
TINY = 1e-30


class Waits:

    def __init__(self, eng):
        self.eng, self.seen = eng, {}

    def __call__(self, sem, n):
        if n > self.seen.get(sem.name, 0):
            self.eng.wait_ge(sem, n)
            self.seen[sem.name] = n


def xattn_ffn_kernel(nc, x, ctx, mask, W_out, scale, log_C,
                     cn_w1, cn_b1, cn_w2, cn_b2, cn_w3, cn_b3, cn_w4, cn_b4,
                     gc_w1, gc_b1, gc_w2, gc_b2, gc_w3, gc_b3, adaptive_range, out):
    NB, S, E = x.shape
    KEYS = ctx.shape[1]
    H, DH = 16, 16
    TT = S // P
    EK = E // P
    PAIRS = H // 2
    HG = 4
    NG = H // HG
    SLOT = 2 * DH
    M2, M3 = cn_w2.shape[1], cn_w3.shape[1]
    G1, G2 = gc_w1.shape[1], gc_w2.shape[1]
    GROUP = 8
    CB = 4
    CT = CB * S
    HALF = CT // 2
    CYCLES = 3
    LAG = 3
    XR = 16
    NLOAD = 4
    BANK = 512
    NGROUPS = NB // GROUP

    with ExitStack() as stack:
        def sb(name, shape, dt=F32):
            return stack.enter_context(nc.sbuf_tensor(name, shape, dt))

        def sem(name):
            return stack.enter_context(nc.semaphore(name))

        ident = sb("ident", [P, P])
        ident16 = sb("ident16", [P, P], F16)
        ones = sb("ones", [P, P])
        wo_in = sb("wo_in", [P, EK, E])
        wo_t = sb("wo_t", [P, EK, E])
        w1 = sb("w1", [P, EK, E])
        w2 = sb("w2", [P, EK, M2])
        w3 = sb("w3", [P, M3])
        w4col = sb("w4col", [P, 1])
        w4rep = sb("w4rep", [P, 2, P])
        g1 = sb("g1", [P, EK, G1])
        g2 = sb("g2", [P, G2])
        g3col = sb("g3col", [P, 1])
        g3rep = sb("g3rep", [P, P])
        b1 = sb("b1", [P, EK])
        b2 = sb("b2", [P, 1])
        b3 = sb("b3", [P, 1])
        gb1 = sb("gb1", [P, 1])
        gb2 = sb("gb2", [P, 1])
        scal = sb("scal", [P, 8])
        half_b4 = sb("half_b4", [P, 1])
        half_gb3 = sb("half_gb3", [P, 1])
        sign = sb("sign", [P, 1])
        sign_ar = sb("sign_ar", [P, 1])
        cs_tok = sb("cs_tok", [P, 1])
        cs_glob = sb("cs_glob", [P, 1])
        cs_base = sb("cs_base", [P, 1])
        clip = sb("clip", [P, 1])
        shift = sb("shift", [P, 1])
        u_scale = sb("u_scale", [P, 1])
        mask_u8 = sb("mask_u8", [NB, KEYS], U8)
        mask_f = sb("mask_f", [NB, KEYS])
        exp_bias = sb("exp_bias", [KEYS, NB])

        xy = sb("xy", [P, XR, TT * E])
        cbuf = sb("cbuf", [KEYS, NLOAD, E])
        va = sb("va", [KEYS, 3, H, SLOT])
        stats1 = sb("stats1", [P, TT, 6])
        mv1 = sb("mv1", [P, 2, TT, 2])
        rstd1 = sb("rstd1", [P, 2, TT])
        var1 = sb("var1", [P, TT])
        var2 = sb("var2", [P, TT])
        minus_half = sb("minus_half", [P, TT])
        q_hat = sb("q_hat", [P, TT, E])
        q_hl = sb("q_hl", [P, 2, TT, PAIRS, 2, 2, 2 * DH], F16)
        k_max = sb("k_max", [KEYS, 1])
        k_amax = sb("k_amax", [KEYS, 1])
        k_inv = sb("k_inv", [KEYS, 1])
        t_scale = sb("t_scale", [KEYS, 4, 1])
        k_hat = sb("k_hat", [KEYS, E])
        kz = sb("kz", [KEYS, 2, H, 2, 2, 2 * DH], F16)
        q_st = sb("q_st", [P, 2, PAIRS, S], F16)
        k_st = sb("k_st", [P, 2, H, KEYS], F16)
        probs = sb("probs", [KEYS, 2, H, S])
        o_t = sb("o_t", [P, 2, NG, S])
        inv_sum = sb("inv_sum", [P, TT, H])
        o_tok = sb("o_tok", [P, TT, E])
        of_t = sb("of_t", [P, EK, S])
        stats2 = sb("stats2", [P, TT, 6])
        mv2 = sb("mv2", [P, TT, 2])
        rstd2 = sb("rstd2", [P, TT])
        f_hat = sb("f_hat", [P, TT, E])

        f_t = sb("f_t", [P, EK, GROUP * S])
        f_sum = sb("f_sum", [P, EK, GROUP])
        h1 = sb("h1", [P, 2, EK, CT])
        h2 = sb("h2", [P, 2, CT])
        h3 = sb("h3", [P, 2, HALF])
        coup = sb("coup", [P, 2, CT])
        move = sb("move", [P, EK, CT])
        gh1 = sb("gh1", [P, GROUP])
        gh2 = sb("gh2", [P, GROUP])
        gth = sb("gth", [P, GROUP])
        cs_batch = sb("cs_batch", [P, GROUP])

        ps = stack.enter_context(nc.psum_tensor("ps", [P, 8, BANK], F32))
        ps_flat = ps[:].rearrange("p b n -> p (b n)")
        SCORE_BANKS = ((0, 1), (2, 3))
        PV_BANKS = (4, 5)
        TR_BANK = 6
        X_BANK = 7

        def banks(first, n=1):
            return ps_flat[:, first * BANK:(first + n) * BANK]

        s_w = sem("s_w")
        s_mask = sem("s_mask")
        s_ldx = [sem(f"s_ldx{n}") for n in range(NLOAD)]
        s_ldc = [sem(f"s_ldc{n}") for n in range(NLOAD)]
        s_st = [sem(f"s_st{n}") for n in range(XR)]
        s_pool0, s_vec0, s_act0, s_pe0 = sem("s_pool0"), sem("s_vec0"), sem("s_act0"), sem("s_pe0")
        s_va = sem("s_va")
        s_stats = sem("s_stats")
        s_mv = sem("s_mv")
        s_var, s_var2 = sem("s_var"), sem("s_var2")
        s_rstd = sem("s_rstd")
        s_qhat = sem("s_qhat")
        s_qhi = sem("s_qhi")
        s_qlo = sem("s_qlo")
        s_qhl, s_kz = sem("s_qhl"), sem("s_kz")
        s_kmax, s_kamax, s_kinv = sem("s_kmax"), sem("s_kamax"), sem("s_kinv")
        s_tsc = sem("s_tsc")
        s_khat, s_khi, s_klo = sem("s_khat"), sem("s_khi"), sem("s_klo")
        s_qtr, s_ktr = sem("s_qtr"), sem("s_ktr")
        s_qst, s_kst = sem("s_qst"), sem("s_kst")
        s_score = sem("s_score")
        s_tanh = sem("s_tanh")
        s_exp = sem("s_exp")
        s_pv = sem("s_pv")
        s_ot = sem("s_ot")
        s_otr = sem("s_otr")
        s_inv = sem("s_inv")
        s_otok = sem("s_otok")
        s_oftr = sem("s_oftr")
        s_oft = sem("s_oft")
        s_proj = sem("s_proj")
        s_y = sem("s_y")
        s_stats2, s_mv2, s_rstd2, s_fhat = sem("s_stats2"), sem("s_mv2"), sem("s_rstd2"), sem("s_fhat")
        s_ftr = sem("s_ftr")
        s_ft = sem("s_ft")
        s_l1 = sem("s_l1")
        s_h1 = sem("s_h1")
        s_l2 = sem("s_l2")
        s_h2 = sem("s_h2")
        s_l3, s_h3 = sem("s_l3"), sem("s_h3")
        s_l4, s_th = sem("s_l4"), sem("s_th")
        s_coup = sem("s_coup")
        s_move = sem("s_move")
        s_upd = sem("s_upd")
        s_glob, s_gact, s_gcs = sem("s_glob"), sem("s_gact"), sem("s_gcs")
        s_back = sem("s_back")
        s_res = sem("s_res")

        n_weights = 0
        block = stack.enter_context(nc.Block())

        def col(ap):
            return ap.rearrange("(p a) -> p a", a=1)

        weight_loads = [
            (wo_in[:], W_out.rearrange("(k p) f -> p k f", p=P)),
            (w1[:], cn_w1.rearrange("(k p) f -> p k f", p=P)),
            (w2[:], cn_w2.rearrange("(k p) f -> p k f", p=P)),
            (w3[:], cn_w3),
            (w4col[0:M3, :], cn_w4), (w4col[M3:P, :], cn_w4),
            (g1[:], gc_w1.rearrange("(k p) f -> p k f", p=P)),
            (g2[:], gc_w2),
            (g3col[0:G2, :], gc_w3),
            (b1[:, 0:1], col(cn_b1[0:P])), (b1[:, 1:2], col(cn_b1[P:E])),
            (b2[:], col(cn_b2)),
            (b3[0:M3, :], col(cn_b3)), (b3[M3:P, :], col(cn_b3)),
            (gb1[:], col(gc_b1)),
            (gb2[0:G2, :], col(gc_b2)),
        ]
        for n, one in enumerate((scale, log_C, cn_b4, gc_b3, adaptive_range)):
            weight_loads.append((scal[:, n:n + 1], one.partition_broadcast(P)))
        n_weights = 16 * len(weight_loads)

        def slots():
            for i in range(-2, NB + LAG + 1):
                yield "attention", i
                done = i - LAG
                if done >= 0 and (done + 1) % GROUP == 0:
                    yield "ffn", done // GROUP

        def passes(g):
            n = g * CYCLES * 2
            for cyc in range(CYCLES):
                yield cyc, n + 2 * cyc, n + 2 * cyc + 1

        @block.sync
        def _(eng):
            wait = Waits(eng)
            eng.dma_start(mask_u8[:], mask.rearrange("b a k -> b (a k)")).then_inc(s_mask, 16)

            def load(b):
                if b >= XR:
                    wait(s_st[b % XR], 16 * (b // XR))
                if b >= NLOAD:
                    wait(s_stats, 2 * (b - NLOAD + 1))
                eng.dma_start(xy[:, b % XR, :], x[b].rearrange("(p t) e -> p (t e)", t=TT)) \
                   .then_inc(s_ldx[b % NLOAD], 16)
                if b >= NLOAD:
                    wait(s_khat, b - NLOAD + 1)
                    wait(s_va, b - NLOAD + 1)
                eng.dma_start(cbuf[:, b % NLOAD, :], ctx[b]).then_inc(s_ldc[b % NLOAD], 16)

            for kind, i in slots():
                if kind == "attention":
                    if i == -2:
                        load(0)
                        load(1)
                        for dst, src in weight_loads:
                            eng.dma_start(dst, src).then_inc(s_w, 16)
                        load(2)
                    elif 0 <= i + 4 < NB and i >= -1:
                        load(i + 4)
                else:
                    for b in range(i * GROUP, (i + 1) * GROUP):
                        wait(s_res, b + 1)
                        eng.dma_start(out[b].rearrange("(p t) e -> p (t e)", t=TT), xy[:, b % XR, :]) \
                           .then_inc(s_st[b % XR], 16)
            for n in range(XR):
                eng.wait_ge(s_st[n], 16 * (NB // XR))

        @block.gpsimd
        def _(eng):
            wait = Waits(eng)
            eng.memset(ident[:], 0.0).then_inc(s_pool0, 1)
            eng.memset(sign[:], 1.0).then_inc(s_pool0, 1)
            eng.wait_ge(s_pool0, 2)
            eng.affine_select(out=ident[:], in_=ident[:], compare_op=ALU.not_equal, fill=1.0, base=0,
                              pattern=[[-1, P]], channel_multiplier=1).then_inc(s_pool0, 1)
            eng.affine_select(out=sign[:], in_=sign[:], compare_op=ALU.is_ge, fill=-1.0, base=P // 2 - 1,
                              pattern=[[0, 1]], channel_multiplier=-1).then_inc(s_pool0, 1)
            eng.memset(ones[:], 1.0).then_inc(s_pool0, 1)
            eng.memset(va[:], 1.0).then_inc(s_pool0, 1)
            eng.memset(kz[:], 0.0).then_inc(s_pool0, 1)
            eng.memset(minus_half[:], -0.5).then_inc(s_pool0, 1)
            wait(s_pool0, 8)

            def prepare(b):
                wait(s_mv, 2 * (b + 1))
                if b >= 2:
                    wait(s_qhat, 2 * (b - 1))
                wait(s_rstd, b)
                eng.tensor_scalar(var1[:], mv1[:, b % 2, :, 1], EPS, None, ALU.add).then_inc(s_var, 1)
                wait(s_var, b + 1)
                eng.tensor_tensor(rstd1[:, b % 2, :], var1[:], minus_half[:], ALU.pow).then_inc(s_rstd, 1)
                wait(s_ldc[b % NLOAD], 16 * (b // NLOAD + 1))
                if b >= 3:
                    wait(s_pv, 2 * (b - 2))
                eng.tensor_scalar(va[:, b % 3, :, 0:DH], cbuf[:, b % NLOAD, :].rearrange("k (h d) -> k h d", d=DH),
                                  1.0, None, ALU.mult).then_inc(s_va, 1)

            for kind, i in slots():
                if kind != "attention":
                    continue
                if i + 2 < NB:
                    prepare(i + 2)
                if 0 <= i - 2 < NB:
                    b = i - 2
                    wait(s_mv2, 2 * (b + 1))
                    wait(s_fhat, 2 * b)
                    eng.tensor_scalar(var2[:], mv2[:, :, 1], EPS, None, ALU.add).then_inc(s_var2, 1)
                    wait(s_var2, b + 1)
                    eng.tensor_tensor(rstd2[:], var2[:], minus_half[:], ALU.pow).then_inc(s_rstd2, 1)

        @block.vector
        def _(eng):
            wait = Waits(eng)
            wait(s_pool0, 8)
            eng.tensor_copy(ident16[:], ident[:]).then_inc(s_vec0, 1)
            wait(s_mask, 16)
            eng.tensor_copy(mask_f[:], mask_u8[:]).then_inc(s_vec0, 1)

            def constants():
                wait(s_w, n_weights)
                eng.memset(w4rep[:], 0.0).then_inc(s_vec0, 1)
                eng.tensor_scalar(half_b4[:], scal[:, 2:3], 0.5, None, ALU.mult).then_inc(s_vec0, 1)
                eng.tensor_scalar(half_gb3[:], scal[:, 3:4], 0.5, None, ALU.mult).then_inc(s_vec0, 1)
                eng.tensor_scalar(sign_ar[:], scal[:, 4:5], sign[:, 0:1], None, ALU.mult).then_inc(s_vec0, 1)
                eng.tensor_scalar(cs_base[:], sign[:], 0.1, None, ALU.mult).then_inc(s_vec0, 1)
                eng.tensor_scalar(u_scale[:], scal[:, 0:1], 1.0 / (Q_SCALE * K_SCALE * DH ** 0.5), None, ALU.mult) \
                   .then_inc(s_vec0, 1)
                eng.tensor_scalar(g3rep[0:G2, :], ones[0:G2, :], g3col[0:G2, 0:1], None, ALU.mult).then_inc(s_vec0, 1)
                wait(s_vec0, 9)
                eng.tensor_scalar(w4rep[0:M3, 0, :], ones[0:M3, :], w4col[0:M3, 0:1], None, ALU.mult).then_inc(s_vec0, 1)
                eng.tensor_scalar(w4rep[M3:P, 1, :], ones[M3:P, :], w4col[M3:P, 0:1], None, ALU.mult).then_inc(s_vec0, 1)
                eng.tensor_scalar(cs_tok[:], sign_ar[:], 0.3, None, ALU.mult).then_inc(s_vec0, 1)
                eng.tensor_scalar(cs_glob[:], sign_ar[:], 0.7, None, ALU.mult).then_inc(s_vec0, 1)
                wait(s_act0, 1)
                eng.tensor_scalar(shift[:], clip[:], -EXP_ROOM, 0.0, ALU.add, ALU.max).then_inc(s_vec0, 1)
                wait(s_pe0, 2)
                eng.tensor_copy(wo_t[:].rearrange("p k e -> p (k e)"), banks(X_BANK)).then_inc(s_vec0, 1)
                wait(s_vec0, 15)
                eng.tensor_scalar(exp_bias[:], banks(TR_BANK)[0:KEYS, 0:NB], MASKED, shift[0:KEYS, 0:1],
                                  ALU.mult, ALU.subtract).then_inc(s_vec0, 1)

            def stats(b):
                wait(s_ldx[b % NLOAD], 16 * (b // NLOAD + 1))
                for t in range(TT):
                    wait(s_mv, 2 * b)
                    eng.bn_stats(stats1[:, t, :], xy[:, b % XR, t * E:(t + 1) * E]).then_inc(s_stats, 1)
                if b >= 2:
                    wait(s_rstd, b - 1)
                    wait(s_qhat, 2 * (b - 1))
                for t in range(TT):
                    wait(s_stats, 2 * b + t + 1)
                    eng.bn_aggr(mv1[:, b % 2, t, :], stats1[:, t, :]).then_inc(s_mv, 1)

            def key_max(b):
                wait(s_ldc[b % NLOAD], 16 * (b // NLOAD + 1))
                wait(s_kamax, b)
                eng.tensor_reduce(k_max[:], cbuf[:, b % NLOAD, :], AX.X, ALU.max, apply_absolute_value=True) \
                   .then_inc(s_kmax, 1)

            def key_scale(b):
                wait(s_kmax, b + 1)
                wait(s_tsc, b)
                eng.tensor_scalar(k_amax[:], k_max[:], TINY, None, ALU.max).then_inc(s_kamax, 1)

            def key_inverse(b):
                wait(s_kamax, b + 1)
                wait(s_khat, b)
                eng.reciprocal(k_inv[:], k_amax[:]).then_inc(s_kinv, 1)
                if b >= 4:
                    wait(s_tanh, NG * (b - 3))
                eng.tensor_scalar(t_scale[:, b % 4, :], k_amax[:], u_scale[0:KEYS, 0:1], 1.0, ALU.mult, ALU.mult) \
                   .then_inc(s_tsc, 1)

            def key_hat(b):
                wait(s_kinv, b + 1)
                wait(s_klo, b)
                eng.tensor_scalar(k_hat[:], cbuf[:, b % NLOAD, :], k_inv[:, 0:1], K_SCALE, ALU.mult, ALU.mult) \
                   .then_inc(s_khat, 1)

            HEAD = 4 * 2 * DH

            def kz_heads(b, part):
                z = kz[:, b % 2, 0, part, 0, :]
                return bass.AP(z.tensor, z.offset, [list(z.ap[0]), [2 * HEAD, PAIRS], [HEAD + DH, 2], [1, DH]])

            def key_high(b):
                wait(s_khat, b + 1)
                if b >= 2:
                    wait(s_ktr, 2 * (b - 1))
                eng.tensor_copy(kz_heads(b, 0), k_hat[:].rearrange("k (p j d) -> k p j d", j=2, d=DH)) \
                   .then_inc(s_khi, 1)

            def key_low(b):
                wait(s_khi, b + 1)
                eng.tensor_tensor(kz_heads(b, 1), k_hat[:].rearrange("k (p j d) -> k p j d", j=2, d=DH),
                                  kz_heads(b, 0), ALU.subtract).then_inc(s_klo, 1)

            def key_twice(b):
                wait(s_klo, b + 1)
                eng.tensor_copy(kz[:, b % 2, :, :, 1, :], kz[:, b % 2, :, :, 0, :]).then_inc(s_kz, 1)

            def query_hat(b):
                wait(s_rstd, b + 1)
                wait(s_qlo, b)
                for t in range(TT):
                    eng.tensor_scalar(q_hat[:, t, :], xy[:, b % XR, t * E:(t + 1) * E],
                                      mv1[:, b % 2, t, 0:1], rstd1[:, b % 2, t:t + 1],
                                      ALU.subtract, ALU.mult).then_inc(s_qhat, 1)

            q_pairs = q_hat[:].rearrange("p t (a d) -> p (t a) d", d=2 * DH)

            def q_part(b, part):
                return q_hl[:, b % 2].rearrange("p t a r h d -> p (t a) r h d")[:, :, 0, part, :]

            def query_high(b):
                wait(s_qhat, 2 * (b + 1))
                if b >= 2:
                    wait(s_qtr, 2 * (b - 1))
                eng.tensor_scalar(q_part(b, 0), q_pairs, Q_SCALE, None, ALU.mult).then_inc(s_qhi, 1)

            def query_low(b):
                wait(s_qhi, b + 1)
                eng.scalar_tensor_tensor(q_part(b, 1), q_pairs, Q_SCALE, q_part(b, 0),
                                         ALU.mult, ALU.subtract).then_inc(s_qlo, 1)

            def query_twice(b):
                wait(s_qlo, b + 1)
                both = q_hl[:, b % 2].rearrange("p t a r h d -> p (t a) r (h d)")
                eng.tensor_copy(both[:, :, 1, :], both[:, :, 0, :]).then_inc(s_qhl, 1)

            def q_stack(b, t):
                wait(s_qtr, 2 * b + t + 1)
                if b >= 2:
                    wait(s_score, NG * (b - 1))
                eng.tensor_copy(q_st[:, b % 2, :, t * P:(t + 1) * P],
                                banks(TR_BANK).bitcast(F16).rearrange("p (a q) -> p a q", q=P)).then_inc(s_qst, 1)

            def k_stack(b, n):
                wait(s_ktr, 2 * b + n + 1)
                if b >= 2:
                    wait(s_score, NG * (b - 1))
                eng.tensor_copy(k_st[:, b % 2, n * PAIRS:(n + 1) * PAIRS, :],
                                banks(TR_BANK).bitcast(F16)[:, 0:PAIRS * KEYS].rearrange("p (a q) -> p a q", q=KEYS)) \
                   .then_inc(s_kst, 1)

            def divide(b):
                for t in range(TT):
                    heads = banks(PV_BANKS[t]).rearrange("p (h s) -> p h s", s=SLOT)
                    wait(s_otr, 2 * b + t + 1)
                    wait(s_otok, 2 * (b - 1) + t + 1)
                    eng.reciprocal(inv_sum[:, t, :], heads[:, :, DH]).then_inc(s_inv, 1)
                for t in range(TT):
                    heads = banks(PV_BANKS[t]).rearrange("p (h s) -> p h s", s=SLOT)
                    wait(s_inv, 2 * b + t + 1)
                    wait(s_oftr, b)
                    eng.tensor_tensor(o_tok[:, t, :].rearrange("p (h d) -> p h d", d=DH), heads[:, :, 0:DH],
                                      inv_sum[:, t, :].unsqueeze(2).to_broadcast([P, H, DH]), ALU.mult) \
                       .then_inc(s_otok, 1)

            def attn_features(b):
                wait(s_oftr, b + 1)
                wait(s_proj, b)
                eng.tensor_copy(of_t[:].rearrange("p k q -> p (k q)"), banks(X_BANK)).then_inc(s_oft, 1)

            def residual(b):
                wait(s_proj, b + 1)
                eng.tensor_tensor(xy[:, b % XR, :], xy[:, b % XR, :], banks(X_BANK), ALU.add).then_inc(s_y, 1)

            def stats_2(b):
                wait(s_y, b + 1)
                wait(s_mv2, 2 * b)
                for t in range(TT):
                    eng.bn_stats(stats2[:, t, :], xy[:, b % XR, t * E:(t + 1) * E]).then_inc(s_stats2, 1)
                wait(s_rstd2, b)
                wait(s_fhat, 2 * b)
                for t in range(TT):
                    wait(s_stats2, 2 * b + t + 1)
                    eng.bn_aggr(mv2[:, t, :], stats2[:, t, :]).then_inc(s_mv2, 1)

            def norm_2(b):
                wait(s_rstd2, b + 1)
                wait(s_ftr, b)
                for t in range(TT):
                    eng.tensor_scalar(f_hat[:, t, :], xy[:, b % XR, t * E:(t + 1) * E],
                                      mv2[:, t, 0:1], rstd2[:, t:t + 1], ALU.subtract, ALU.mult).then_inc(s_fhat, 1)

            def update(g, chunk, n):
                wait(s_th, n + 1)
                wait(s_gcs, g + 1)
                for b in range(CB):
                    c = coup[:, chunk, b * S:(b + 1) * S]
                    eng.tensor_scalar(c, c, cs_tok[:, 0:1], cs_batch[:, chunk * CB + b:chunk * CB + b + 1],
                                      ALU.mult, ALU.add).then_inc(s_coup, 1)
                wait(s_coup, CB * (n + 1))
                wait(s_upd, 2 * n)
                tok = slice(chunk * CT, (chunk + 1) * CT)
                for k in range(EK):
                    eng.tensor_tensor(move[:, k, :], f_t[:, 1 - k, tok], coup[:, chunk, :], ALU.mult) \
                       .then_inc(s_move, 1)
                for k in range(EK):
                    wait(s_move, 2 * n + EK)
                    eng.tensor_tensor(f_t[:, k, tok], f_t[:, k, tok], move[:, k, :],
                                      (ALU.add, ALU.subtract)[k]).then_inc(s_upd, 1)

            def results(b):
                wait(s_back, b + 1)
                eng.tensor_tensor(xy[:, b % XR, :], xy[:, b % XR, :], banks(PV_BANKS[b % 2]), ALU.add) \
                   .then_inc(s_res, 1)

            late = []
            for kind, i in slots():
                if kind == "attention":
                    new, nxt, old = i + 2, i + 1, i - 2
                    fresh, ahead, past = new < NB, 0 <= nxt < NB, 0 <= old < NB
                    for b in late:
                        results(b)
                    late = []
                    if ahead:
                        q_stack(nxt, 0)
                    if past:
                        divide(old)
                    if fresh:
                        stats(new)
                        key_max(new)
                    if i == -2:
                        constants()
                    if ahead:
                        q_stack(nxt, 1)
                    if past:
                        attn_features(old)
                    if fresh:
                        key_scale(new)
                        query_hat(new)
                        key_inverse(new)
                    if ahead:
                        k_stack(nxt, 0)
                    if fresh:
                        key_hat(new)
                        query_high(new)
                    if past:
                        residual(old)
                    if fresh:
                        key_high(new)
                    if past:
                        stats_2(old)
                    if ahead:
                        k_stack(nxt, 1)
                    if fresh:
                        query_low(new)
                        key_low(new)
                        query_twice(new)
                        key_twice(new)
                    if past:
                        norm_2(old)
                else:
                    for cyc, na, nb in passes(i):
                        if cyc == 0:
                            wait(s_gact, 3 * (i + 1))
                            eng.tensor_scalar(cs_batch[:], gth[:], cs_glob[:, 0:1], cs_base[:, 0:1],
                                              ALU.mult, ALU.add).then_inc(s_gcs, 1)
                            wait(s_gcs, i + 1)
                        update(i, 0, na)
                        update(i, 1, nb)
                    for b in range(i * GROUP, i * GROUP + CB):
                        results(b)
                    late = list(range(i * GROUP + CB, (i + 1) * GROUP))
            for b in late:
                results(b)

        @block.scalar
        def _(eng):
            wait = Waits(eng)
            wait(s_w, n_weights)
            eng.activation(clip[:], scal[:, 1:2], ACT.Exp).then_inc(s_act0, 1)

            def tanh(b, n):
                wait(s_score, NG * b + n + 1)
                wait(s_tsc, b + 1)
                if b >= 2:
                    wait(s_pv, 2 * (b - 2) + n // 2 + 1)
                first = SCORE_BANKS[n % 2][0]
                eng.activation(probs[:, b % 2, n * HG:(n + 1) * HG, :].rearrange("k h q -> k (h q)"),
                               banks(first, 2)[0:KEYS, :], ACT.Tanh, scale=t_scale[:, b % 4, :]).then_inc(s_tanh, 1)

            def exp(b, n):
                wait(s_tanh, NG * b + 2 * n + 2)
                p = probs[:, b % 2, 2 * n * HG:2 * (n + 1) * HG, :].rearrange("k h q -> k (h q)")
                eng.activation(p, p, ACT.Exp, scale=clip[0:KEYS, 0:1], bias=exp_bias[:, b:b + 1]).then_inc(s_exp, 1)

            def attn_out(b, n):
                wait(s_pv, 2 * b + n + 1)
                if b >= 2:
                    wait(s_otr, 2 * (b - 1))
                eng.activation(o_t[:, b % 2, 2 * n:2 * n + 2, :].rearrange("p c q -> p (c q)"),
                               banks(PV_BANKS[n]), ACT.Copy).then_inc(s_ot, 1)

            def features(b):
                wait(s_ftr, b + 1)
                if b >= GROUP:
                    g = b // GROUP
                    wait(s_back, g * GROUP)
                    wait(s_glob, 3 * g)
                at = b % GROUP
                for k in range(EK):
                    eng.activation(f_t[:, k, at * S:(at + 1) * S], banks(X_BANK)[:, k * S:(k + 1) * S],
                                   ACT.Identity, accum_out=f_sum[:, k, at:at + 1]).then_inc(s_ft, 1)

            def gelu1(n, chunk):
                for m in range(EK):
                    wait(s_l1, 2 * n + m + 1)
                    if n >= 2:
                        wait(s_l2, 2 * (n - 1))
                    eng.activation(h1[:, chunk, m, :], banks(SCORE_BANKS[m][0], 2), ACT.Gelu, bias=b1[:, m:m + 1]) \
                       .then_inc(s_h1, 1)

            def gelu2(n, chunk, half):
                wait(s_l2, 2 * n + half + 1)
                if n >= 2:
                    wait(s_l3, n - 1)
                eng.activation(h2[:, chunk, half * HALF:(half + 1) * HALF], banks(PV_BANKS[half]), ACT.Gelu,
                               bias=b2[:, 0:1]).then_inc(s_h2, 1)

            def gelu3(n, chunk):
                wait(s_l3, n + 1)
                if n >= 2:
                    wait(s_l4, n - 1)
                eng.activation(h3[:, chunk, :], banks(X_BANK), ACT.Gelu, bias=b3[:, 0:1]).then_inc(s_h3, 1)

            def token_tanh(n, chunk):
                wait(s_l4, n + 1)
                if n >= 2:
                    wait(s_move, 2 * (n - 1))
                eng.activation(coup[:, chunk, :], banks(TR_BANK, 2), ACT.Tanh, scale=0.5, bias=half_b4[:, 0:1]) \
                   .then_inc(s_th, 1)

            wait(s_vec0, 16)
            for kind, i in slots():
                if kind == "attention":
                    on, past = 0 <= i < NB, 0 <= i - 1 < NB
                    for n in range(2):
                        if on:
                            tanh(i, 2 * n)
                        if n == 0 and 0 <= i - LAG < NB:
                            features(i - LAG)
                        if on:
                            tanh(i, 2 * n + 1)
                            exp(i, n)
                        if past:
                            attn_out(i - 1, n)
                else:
                    glob = banks(TR_BANK)
                    for cyc, na, nb in passes(i):
                        gelu1(na, 0)
                        if cyc == 0:
                            wait(s_glob, 3 * i + 1)
                            eng.activation(gh1[:], glob[:, 0:GROUP], ACT.Gelu, bias=gb1[:, 0:1], scale=1.0 / S) \
                               .then_inc(s_gact, 1)
                        gelu1(nb, 1)
                        if cyc == 0:
                            wait(s_glob, 3 * i + 2)
                            eng.activation(gh2[0:G2, :], glob[0:G2, GROUP:2 * GROUP], ACT.Gelu, bias=gb2[0:G2, 0:1]) \
                               .then_inc(s_gact, 1)
                        gelu2(na, 0, 0)
                        gelu2(na, 0, 1)
                        if cyc == 0:
                            wait(s_glob, 3 * i + 3)
                            if i:
                                wait(s_gcs, i)
                            eng.activation(gth[:], glob[:, 2 * GROUP:3 * GROUP], ACT.Tanh, scale=0.5,
                                           bias=half_gb3[:, 0:1]).then_inc(s_gact, 1)
                        gelu3(na, 0)
                        gelu2(nb, 1, 0)
                        token_tanh(na, 0)
                        gelu2(nb, 1, 1)
                        gelu3(nb, 1)
                        token_tanh(nb, 1)

        @block.tensor
        def _(eng):
            wait = Waits(eng)
            reader = {}

            def claim(*which):
                for bank in which:
                    if bank in reader:
                        wait(*reader[bank])

            def read_by(s, n, *which):
                for bank in which:
                    reader[bank] = (s, n)

            wait(s_pool0, 4)
            wait(s_w, n_weights)
            for k in range(EK):
                for m in range(EK):
                    last = eng.transpose(banks(X_BANK)[:, k * E + m * P:k * E + (m + 1) * P],
                                         wo_in[:, m, k * P:(k + 1) * P], ident[:])
            last.then_inc(s_pe0, 1)
            wait(s_vec0, 2)
            eng.transpose(banks(TR_BANK)[0:KEYS, 0:NB], mask_f[:], ident[0:NB, 0:NB]).then_inc(s_pe0, 1)
            read_by(s_vec0, 16, X_BANK, TR_BANK)

            def query_stack(b, t):
                wait(s_qhl, b + 1)
                claim(TR_BANK)
                dst = banks(TR_BANK).bitcast(F16)
                for pair in range(PAIRS):
                    last = eng.transpose(dst[:, pair * P:(pair + 1) * P],
                                         q_hl[:, b % 2, t, pair].rearrange("p r h d -> p (r h d)"), ident16[:])
                last.then_inc(s_qtr, 1)
                read_by(s_qst, 2 * b + t + 1, TR_BANK)

            def key_stack(b, n):
                wait(s_kz, b + 1)
                claim(TR_BANK)
                dst = banks(TR_BANK).bitcast(F16)
                for j in range(PAIRS):
                    last = eng.transpose(dst[:, j * KEYS:(j + 1) * KEYS],
                                         kz[:, b % 2, n * PAIRS + j].rearrange("k h r d -> k (h r d)"),
                                         ident16[0:KEYS, 0:KEYS])
                last.then_inc(s_ktr, 1)
                read_by(s_kst, 2 * b + n + 1, TR_BANK)

            def scores(b, n):
                wait(s_qst, 2 * (b + 1))
                wait(s_kst, 2 * b + n // 2 + 1)
                pair_of_banks = SCORE_BANKS[n % 2]
                claim(*pair_of_banks)
                for j in range(HG):
                    h = n * HG + j
                    last = eng.matmul(banks(pair_of_banks[0], 2)[0:KEYS, j * S:(j + 1) * S],
                                      k_st[:, b % 2, h, :], q_st[:, b % 2, h // 2, :], start=True, stop=True)
                last.then_inc(s_score, 1)
                read_by(s_tanh, NG * b + n + 1, *pair_of_banks)

            def weighted_values(b, n):
                wait(s_exp, 2 * b + n + 1)
                wait(s_va, b + 1)
                claim(PV_BANKS[n])
                for c in (2 * n, 2 * n + 1):
                    for j in range(HG):
                        h = c * HG + j
                        last = eng.matmul(banks(PV_BANKS[n])[j * SLOT:(j + 1) * SLOT, (c % 2) * S:(c % 2 + 1) * S],
                                          va[:, b % 3, h, :], probs[:, b % 2, h, :], start=True, stop=True,
                                          tile_position=(0, j * SLOT))
                last.then_inc(s_pv, 1)
                read_by(s_ot, 2 * b + n + 1, PV_BANKS[n])

            def attn_to_tokens(b):
                wait(s_ot, 2 * (b + 1))
                for t in range(TT):
                    claim(PV_BANKS[t])
                    for c in range(NG):
                        last = eng.transpose(banks(PV_BANKS[t])[:, c * P:(c + 1) * P],
                                             o_t[:, b % 2, c, t * P:(t + 1) * P], ident[:])
                    last.then_inc(s_otr, 1)
                    read_by(s_otok, 2 * b + t + 1, PV_BANKS[t])

            def attn_to_features(b):
                wait(s_otok, 2 * (b + 1))
                claim(X_BANK)
                for k in range(EK):
                    for t in range(TT):
                        last = eng.transpose(banks(X_BANK)[:, k * S + t * P:k * S + (t + 1) * P],
                                             o_tok[:, t, k * P:(k + 1) * P], ident[:])
                last.then_inc(s_oftr, 1)
                read_by(s_oft, b + 1, X_BANK)

            def project(b):
                wait(s_oft, b + 1)
                claim(X_BANK)
                for t in range(TT):
                    for k in range(EK):
                        last = eng.matmul(banks(X_BANK)[:, t * E:(t + 1) * E], of_t[:, k, t * P:(t + 1) * P],
                                          wo_t[:, k, :], start=(k == 0), stop=(k == EK - 1))
                last.then_inc(s_proj, 1)
                read_by(s_y, b + 1, X_BANK)

            def norm_to_features(b):
                wait(s_fhat, 2 * (b + 1))
                claim(X_BANK)
                for k in range(EK):
                    for t in range(TT):
                        last = eng.transpose(banks(X_BANK)[:, k * S + t * P:k * S + (t + 1) * P],
                                             f_hat[:, t, k * P:(k + 1) * P], ident[:])
                last.then_inc(s_ftr, 1)
                read_by(s_ft, 2 * (b + 1), X_BANK)

            def layer1(g, n, chunk):
                if n >= 2 * CYCLES * g + 2:
                    wait(s_upd, 2 * (n - 1))
                else:
                    wait(s_ft, 2 * (g * GROUP + (chunk + 1) * CB))
                for m in range(EK):
                    pair_of_banks = SCORE_BANKS[m]
                    claim(*pair_of_banks)
                    for half in range(2):
                        for k in range(EK):
                            tok = chunk * CT + half * HALF
                            last = eng.matmul(banks(pair_of_banks[half]), w1[:, k, m * P:(m + 1) * P],
                                              f_t[:, k, tok:tok + HALF], start=(k == 0), stop=(k == EK - 1))
                    last.then_inc(s_l1, 1)
                    read_by(s_h1, 2 * n + m + 1, *pair_of_banks)

            def layer2(n, chunk, half):
                wait(s_h1, 2 * (n + 1))
                claim(PV_BANKS[half])
                for k in range(EK):
                    last = eng.matmul(banks(PV_BANKS[half]), w2[:, k, :], h1[:, chunk, k, half * HALF:(half + 1) * HALF],
                                      start=(k == 0), stop=(k == EK - 1))
                last.then_inc(s_l2, 1)
                read_by(s_h2, 2 * n + half + 1, PV_BANKS[half])

            def layer3(n, chunk):
                wait(s_h2, 2 * (n + 1))
                claim(X_BANK)
                for half in range(2):
                    last = eng.matmul(banks(X_BANK)[half * M3:(half + 1) * M3, :], w3[:],
                                      h2[:, chunk, half * HALF:(half + 1) * HALF], start=True, stop=True,
                                      tile_position=(0, half * M3))
                last.then_inc(s_l3, 1)
                read_by(s_h3, n + 1, X_BANK)

            def layer4(n, chunk):
                wait(s_h3, n + 1)
                claim(TR_BANK, X_BANK)
                for half in range(2):
                    last = eng.matmul(banks(TR_BANK + half), w4rep[:, half, :], h3[:, chunk, :], start=True, stop=True)
                last.then_inc(s_l4, 1)
                read_by(s_th, n + 1, TR_BANK, X_BANK)

            def global_net(g, layer):
                dst = banks(TR_BANK)
                if layer == 0:
                    wait(s_ft, 2 * (g + 1) * GROUP)
                    claim(TR_BANK)
                    for k in range(EK):
                        last = eng.matmul(dst[:, 0:GROUP], g1[:, k, :], f_sum[:, k, :], start=(k == 0), stop=(k == EK - 1))
                else:
                    wait(s_gact, 3 * g + layer)
                    if layer == 1:
                        last = eng.matmul(dst[0:G2, GROUP:2 * GROUP], g2[:], gh1[:], start=True, stop=True)
                    else:
                        last = eng.matmul(dst[:, 2 * GROUP:3 * GROUP], g3rep[0:G2, :], gh2[0:G2, :],
                                          start=True, stop=True)
                last.then_inc(s_glob, 1)
                read_by(s_gact, 3 * g + layer + 1, TR_BANK)

            def to_tokens(b, n):
                wait(s_upd, 2 * (n + 1))
                bank, at = PV_BANKS[b % 2], b % GROUP
                claim(bank)
                for t in range(TT):
                    for k in range(EK):
                        last = eng.transpose(banks(bank)[:, t * E + k * P:t * E + (k + 1) * P],
                                             f_t[:, k, at * S + t * P:at * S + (t + 1) * P], ident[:])
                last.then_inc(s_back, 1)
                read_by(s_res, b + 1, bank)

            late = []
            for kind, i in slots():
                if kind == "attention":
                    nxt, done, old = i + 1, i - 1, i - 2
                    on, ahead, past, older = 0 <= i < NB, 0 <= nxt < NB, 0 <= done < NB, 0 <= old < NB
                    if on:
                        scores(i, 0)
                    for b, n in late:
                        to_tokens(b, n)
                    late = []
                    if ahead:
                        query_stack(nxt, 0)
                    if older:
                        attn_to_tokens(old)
                    if 0 <= i - LAG < NB:
                        norm_to_features(i - LAG)
                    if on:
                        scores(i, 1)
                    if ahead:
                        query_stack(nxt, 1)
                    if older:
                        attn_to_features(old)
                    if past:
                        weighted_values(done, 0)
                    if on:
                        scores(i, 2)
                    if ahead:
                        key_stack(nxt, 0)
                    if older:
                        project(old)
                    if past:
                        weighted_values(done, 1)
                    if on:
                        scores(i, 3)
                    if ahead:
                        key_stack(nxt, 1)
                else:
                    for cyc, na, nb in passes(i):
                        layer1(i, na, 0)
                        if cyc == 0:
                            global_net(i, 0)
                        layer1(i, nb, 1)
                        if cyc == 0:
                            global_net(i, 1)
                        layer2(na, 0, 0)
                        layer2(na, 0, 1)
                        if cyc == 0:
                            global_net(i, 2)
                        layer3(na, 0)
                        layer2(nb, 1, 0)
                        layer4(na, 0)
                        layer2(nb, 1, 1)
                        layer3(nb, 1)
                        layer4(nb, 1)
                    first = i * GROUP
                    for b in range(first, first + CB):
                        to_tokens(b, na)
                    late = [(b, nb) for b in range(first + CB, first + GROUP)]
            for b, n in late:
                to_tokens(b, n)


_INS = ['x', 'ctx_1024', 'mask_Bx1xS2_bk0', 'L0_xattn_W_out', 'L0_xattn_scale', 'L0_xattn_log_C',
        'L0_ffn_cn_w1', 'L0_ffn_cn_b1', 'L0_ffn_cn_w2', 'L0_ffn_cn_b2', 'L0_ffn_cn_w3', 'L0_ffn_cn_b3',
        'L0_ffn_cn_w4', 'L0_ffn_cn_b4', 'L0_ffn_gc_w1', 'L0_ffn_gc_b1', 'L0_ffn_gc_w2', 'L0_ffn_gc_b2',
        'L0_ffn_gc_w3', 'L0_ffn_gc_b3', 'L0_ffn_adaptive_range']


def kernel(**inputs):
    import numpy as _np
    import concourse.bacc as _bacc
    from concourse import mybir as _mybir
    from concourse.bass_utils import run_bass_kernel_spmd as _run

    nc = _bacc.Bacc("TRN2", target_bir_lowering=False, num_devices=1)
    arrays, args = {}, []
    for name in _INS:
        a = _np.ascontiguousarray(inputs[name])
        a = a.reshape(a.shape or (1,))
        arrays[f"in_{name}_dram"] = a
        args.append(nc.dram_tensor(f"in_{name}_dram", a.shape, _mybir.dt.from_np(a.dtype), kind="ExternalInput").ap())
    shape = tuple(inputs['x'].shape)
    args.append(nc.dram_tensor("out_0_dram", shape, _mybir.dt.float32, kind="ExternalOutput").ap())
    xattn_ffn_kernel(nc, *args)
    r = _run(nc, [arrays], core_ids=[0])
    return r.results[0]["out_0_dram"]
```

```python
from contextlib import ExitStack

import concourse.bass as bass
from concourse import mybir

ALU = mybir.AluOpType
ACT = mybir.ActivationFunctionType
AX = mybir.AxisListType
F32 = mybir.dt.float32
F16 = mybir.dt.float16
U8 = mybir.dt.uint8

P = 128
EPS = 1e-5
MASKED = -1e30
EXP_ROOM = 64.0
Q_SCALE = 256.0
K_SCALE = 256.0
TINY = 1e-30


class Waits:

    def __init__(self, eng):
        self.eng, self.seen = eng, {}

    def __call__(self, sem, n):
        if n > self.seen.get(sem.name, 0):
            self.eng.wait_ge(sem, n)
            self.seen[sem.name] = n


def xattn_ffn_kernel(nc, x, ctx, mask, W_out, scale, log_C,
                     cn_w1, cn_b1, cn_w2, cn_b2, cn_w3, cn_b3, cn_w4, cn_b4,
                     gc_w1, gc_b1, gc_w2, gc_b2, gc_w3, gc_b3, adaptive_range, out):
    NB, S, E = x.shape
    KEYS = ctx.shape[1]
    H, DH = 16, 16
    TT = S // P
    EK = E // P
    PAIRS = H // 2
    HG = 4
    NG = H // HG
    SLOT = 2 * DH
    M2, M3 = cn_w2.shape[1], cn_w3.shape[1]
    G1, G2 = gc_w1.shape[1], gc_w2.shape[1]
    GROUP = 8
    CB = 4
    CT = CB * S
    HALF = CT // 2
    CYCLES = 3
    NORM_LAG = 3
    LAG = 4
    XR = 16
    NLOAD = 4
    BANK = 512
    NGROUPS = NB // GROUP

    with ExitStack() as stack:
        def sb(name, shape, dt=F32):
            return stack.enter_context(nc.sbuf_tensor(name, shape, dt))

        def sem(name):
            return stack.enter_context(nc.semaphore(name))

        ident = sb("ident", [P, P])
        ident16 = sb("ident16", [P, P], F16)
        ones = sb("ones", [P, P])
        wo_in = sb("wo_in", [P, EK, E])
        wo_t = sb("wo_t", [P, EK, E])
        w1 = sb("w1", [P, EK, E])
        w2 = sb("w2", [P, EK, M2])
        w3 = sb("w3", [P, M3])
        w4col = sb("w4col", [P, 1])
        w4rep = sb("w4rep", [P, 2, P])
        g1 = sb("g1", [P, EK, G1])
        g2 = sb("g2", [P, G2])
        g3col = sb("g3col", [P, 1])
        g3rep = sb("g3rep", [P, P])
        b1 = sb("b1", [P, EK])
        b2 = sb("b2", [P, 1])
        b3 = sb("b3", [P, 1])
        gb1 = sb("gb1", [P, 1])
        gb2 = sb("gb2", [P, 1])
        scal = sb("scal", [P, 8])
        half_b4 = sb("half_b4", [P, 1])
        half_gb3 = sb("half_gb3", [P, 1])
        sign = sb("sign", [P, 1])
        sign_ar = sb("sign_ar", [P, 1])
        cs_tok = sb("cs_tok", [P, 1])
        cs_glob = sb("cs_glob", [P, 1])
        cs_base = sb("cs_base", [P, 1])
        clip = sb("clip", [P, 1])
        shift = sb("shift", [P, 1])
        u_scale = sb("u_scale", [P, 1])
        mask_u8 = sb("mask_u8", [NB, KEYS], U8)
        mask_f = sb("mask_f", [NB, KEYS])
        exp_bias = sb("exp_bias", [KEYS, NB])

        xy = sb("xy", [P, XR, TT * E])
        cbuf = sb("cbuf", [KEYS, NLOAD, E])
        va = sb("va", [KEYS, 3, H, SLOT])
        stats1 = sb("stats1", [P, TT, 6])
        mv1 = sb("mv1", [P, 2, TT, 2])
        rstd1 = sb("rstd1", [P, 2, TT])
        var1 = sb("var1", [P, TT])
        var2 = sb("var2", [P, TT])
        neg_mean1 = sb("neg_mean1", [P, TT])
        neg_mean2 = sb("neg_mean2", [P, TT])
        minus_half = sb("minus_half", [P, TT])
        q_hat = sb("q_hat", [P, TT, E])
        q_hl = sb("q_hl", [P, 2, TT, PAIRS, 2, 2, 2 * DH], F16)
        k_max = sb("k_max", [KEYS, 1])
        k_amax = sb("k_amax", [KEYS, 1])
        k_inv = sb("k_inv", [KEYS, 1])
        t_scale = sb("t_scale", [KEYS, 4, 1])
        k_hat = sb("k_hat", [KEYS, E])
        kz = sb("kz", [KEYS, 2, H, 2, 2, 2 * DH], F16)
        q_st = sb("q_st", [P, 2, PAIRS, S], F16)
        k_st = sb("k_st", [P, 2, H, KEYS], F16)
        probs = sb("probs", [KEYS, 2, H, S])
        o_t = sb("o_t", [P, 2, NG, S])
        inv_sum = sb("inv_sum", [P, TT, H])
        o_tok = sb("o_tok", [P, TT, E])
        of_t = sb("of_t", [P, EK, S])
        stats2 = sb("stats2", [P, TT, 6])
        mv2 = sb("mv2", [P, TT, 2])
        rstd2 = sb("rstd2", [P, TT])
        f_hat = sb("f_hat", [P, TT, E])

        f_t = sb("f_t", [P, EK, GROUP * S])
        f_sum = sb("f_sum", [P, EK, GROUP])
        h1 = sb("h1", [P, 2, EK, CT])
        h2 = sb("h2", [P, 2, CT])
        h3 = sb("h3", [P, 2, HALF])
        coup = sb("coup", [P, 2, CT])
        move = sb("move", [P, EK, CT])
        gh1 = sb("gh1", [P, GROUP])
        gh2 = sb("gh2", [P, GROUP])
        gth = sb("gth", [P, GROUP])
        cs_batch = sb("cs_batch", [P, GROUP])

        ps = stack.enter_context(nc.psum_tensor("ps", [P, 8, BANK], F32))
        ps_flat = ps[:].rearrange("p b n -> p (b n)")
        SCORE_BANKS = ((0, 1), (2, 3))
        PV_BANKS = (4, 5)
        TR_BANK = 6
        X_BANK = 7
        L3_BANKS = (6, 5)
        L4_BANKS = (6, 4)

        def banks(first, n=1):
            return ps_flat[:, first * BANK:(first + n) * BANK]

        s_w = sem("s_w")
        s_mask = sem("s_mask")
        s_ldx = [sem(f"s_ldx{n}") for n in range(NLOAD)]
        s_ldc = [sem(f"s_ldc{n}") for n in range(NLOAD)]
        s_st = [sem(f"s_st{n}") for n in range(XR)]
        s_pool0, s_vec0, s_act0, s_pe0 = sem("s_pool0"), sem("s_vec0"), sem("s_act0"), sem("s_pe0")
        s_va = sem("s_va")
        s_stats = sem("s_stats")
        s_mv = sem("s_mv")
        s_var, s_var2 = sem("s_var"), sem("s_var2")
        s_mean, s_mean2 = sem("s_mean"), sem("s_mean2")
        s_rstd = sem("s_rstd")
        s_qhat = sem("s_qhat")
        s_qhi = sem("s_qhi")
        s_qlo = sem("s_qlo")
        s_qhl, s_kz = sem("s_qhl"), sem("s_kz")
        s_kmax, s_kamax, s_kinv = sem("s_kmax"), sem("s_kamax"), sem("s_kinv")
        s_tsc = sem("s_tsc")
        s_khat, s_khi, s_klo = sem("s_khat"), sem("s_khi"), sem("s_klo")
        s_qtr, s_ktr = sem("s_qtr"), sem("s_ktr")
        s_qst, s_kst = sem("s_qst"), sem("s_kst")
        s_score = sem("s_score")
        s_tanh = sem("s_tanh")
        s_exp = sem("s_exp")
        s_pv = sem("s_pv")
        s_ot = sem("s_ot")
        s_otr = sem("s_otr")
        s_inv = sem("s_inv")
        s_otok = sem("s_otok")
        s_oftr = sem("s_oftr")
        s_oft = sem("s_oft")
        s_proj = sem("s_proj")
        s_y = sem("s_y")
        s_stats2, s_mv2, s_rstd2, s_fhat = sem("s_stats2"), sem("s_mv2"), sem("s_rstd2"), sem("s_fhat")
        s_ftr = sem("s_ftr")
        s_ft = sem("s_ft")
        s_l1 = sem("s_l1")
        s_h1 = sem("s_h1")
        s_l2 = sem("s_l2")
        s_h2 = sem("s_h2")
        s_l3, s_h3 = sem("s_l3"), sem("s_h3")
        s_l4, s_th = sem("s_l4"), sem("s_th")
        s_coup = sem("s_coup")
        s_move = sem("s_move")
        s_upd = sem("s_upd")
        s_glob, s_gact, s_gcs = sem("s_glob"), sem("s_gact"), sem("s_gcs")
        s_back = sem("s_back")
        s_res = sem("s_res")

        n_weights = 0
        block = stack.enter_context(nc.Block())

        def col(ap):
            return ap.rearrange("(p a) -> p a", a=1)

        weight_loads = [
            (wo_in[:], W_out.rearrange("(k p) f -> p k f", p=P)),
            (w1[:], cn_w1.rearrange("(k p) f -> p k f", p=P)),
            (w2[:], cn_w2.rearrange("(k p) f -> p k f", p=P)),
            (w3[:], cn_w3),
            (w4col[0:M3, :], cn_w4), (w4col[M3:P, :], cn_w4),
            (g1[:], gc_w1.rearrange("(k p) f -> p k f", p=P)),
            (g2[:], gc_w2),
            (g3col[0:G2, :], gc_w3),
            (b1[:, 0:1], col(cn_b1[0:P])), (b1[:, 1:2], col(cn_b1[P:E])),
            (b2[:], col(cn_b2)),
            (b3[0:M3, :], col(cn_b3)), (b3[M3:P, :], col(cn_b3)),
            (gb1[:], col(gc_b1)),
            (gb2[0:G2, :], col(gc_b2)),
        ]
        for n, one in enumerate((scale, log_C, cn_b4, gc_b3, adaptive_range)):
            weight_loads.append((scal[:, n:n + 1], one.partition_broadcast(P)))
        n_weights = 16 * len(weight_loads)

        def slots():
            for i in range(-2, NB + LAG + 1):
                yield "attention", i
                done = i - LAG
                if done >= 0 and (done + 1) % GROUP == 0:
                    yield "ffn", done // GROUP

        def passes(g):
            n = g * CYCLES * 2
            for cyc in range(CYCLES):
                yield cyc, n + 2 * cyc, n + 2 * cyc + 1

        @block.sync
        def _(eng):
            wait = Waits(eng)
            eng.dma_start(mask_u8[:], mask.rearrange("b a k -> b (a k)")).then_inc(s_mask, 16)

            def load(b):
                if b >= XR:
                    wait(s_st[b % XR], 16 * (b // XR))
                if b >= NLOAD:
                    wait(s_stats, 2 * (b - NLOAD + 1))
                eng.dma_start(xy[:, b % XR, :], x[b].rearrange("(p t) e -> p (t e)", t=TT)) \
                   .then_inc(s_ldx[b % NLOAD], 16)
                if b >= NLOAD:
                    wait(s_khat, b - NLOAD + 1)
                    wait(s_va, b - NLOAD + 1)
                eng.dma_start(cbuf[:, b % NLOAD, :], ctx[b]).then_inc(s_ldc[b % NLOAD], 16)

            def store(b):
                wait(s_res, b + 1)
                eng.dma_start(out[b].rearrange("(p t) e -> p (t e)", t=TT), xy[:, b % XR, :]) \
                   .then_inc(s_st[b % XR], 16)

            late = []
            for kind, i in slots():
                if kind != "attention":
                    late = list(range(i * GROUP, (i + 1) * GROUP))
                    continue
                for b in late[:2]:
                    store(b)
                late = late[2:]
                if i == -2:
                    load(0)
                    load(1)
                    for dst, src in weight_loads:
                        eng.dma_start(dst, src).then_inc(s_w, 16)
                    load(2)
                elif 0 <= i + 4 < NB and i >= -1:
                    load(i + 4)
            for b in late:
                store(b)
            for n in range(XR):
                eng.wait_ge(s_st[n], 16 * (NB // XR))

        @block.gpsimd
        def _(eng):
            wait = Waits(eng)
            eng.memset(ident[:], 0.0).then_inc(s_pool0, 1)
            eng.memset(sign[:], 1.0).then_inc(s_pool0, 1)
            eng.wait_ge(s_pool0, 2)
            eng.affine_select(out=ident[:], in_=ident[:], compare_op=ALU.not_equal, fill=1.0, base=0,
                              pattern=[[-1, P]], channel_multiplier=1).then_inc(s_pool0, 1)
            eng.affine_select(out=sign[:], in_=sign[:], compare_op=ALU.is_ge, fill=-1.0, base=P // 2 - 1,
                              pattern=[[0, 1]], channel_multiplier=-1).then_inc(s_pool0, 1)
            eng.memset(ones[:], 1.0).then_inc(s_pool0, 1)
            eng.memset(va[:], 1.0).then_inc(s_pool0, 1)
            eng.memset(kz[:], 0.0).then_inc(s_pool0, 1)
            eng.memset(minus_half[:], -0.5).then_inc(s_pool0, 1)
            wait(s_pool0, 8)

            def prepare(b):
                wait(s_mv, 2 * (b + 1))
                if b >= 2:
                    wait(s_qhat, 2 * (b - 1))
                wait(s_rstd, b)
                eng.tensor_scalar(var1[:], mv1[:, b % 2, :, 1], EPS, None, ALU.add).then_inc(s_var, 1)
                wait(s_qhat, 2 * b)
                eng.tensor_scalar(neg_mean1[:], mv1[:, b % 2, :, 0], -1.0, None, ALU.mult).then_inc(s_mean, 1)
                wait(s_var, b + 1)
                eng.tensor_tensor(rstd1[:, b % 2, :], var1[:], minus_half[:], ALU.pow).then_inc(s_rstd, 1)

            def values(b):
                wait(s_ldc[b % NLOAD], 16 * (b // NLOAD + 1))
                if b >= 3:
                    wait(s_pv, 2 * (b - 2))
                eng.tensor_scalar(va[:, b % 3, :, 0:DH], cbuf[:, b % NLOAD, :].rearrange("k (h d) -> k h d", d=DH),
                                  1.0, None, ALU.mult).then_inc(s_va, 1)

            def query_hat(b):
                wait(s_rstd, b + 1)
                wait(s_mean, b + 1)
                wait(s_qlo, b)
                for t in range(TT):
                    eng.tensor_scalar(q_hat[:, t, :], xy[:, b % XR, t * E:(t + 1) * E],
                                      neg_mean1[:, t:t + 1], rstd1[:, b % 2, t:t + 1],
                                      ALU.add, ALU.mult).then_inc(s_qhat, 1)

            def key_hat(b):
                wait(s_kinv, b + 1)
                wait(s_klo, b)
                eng.tensor_scalar(k_hat[:], cbuf[:, b % NLOAD, :], k_inv[:, 0:1], K_SCALE, ALU.mult, ALU.mult) \
                   .then_inc(s_khat, 1)

            def norm_2(b):
                wait(s_mv2, 2 * (b + 1))
                wait(s_fhat, 2 * b)
                eng.tensor_scalar(var2[:], mv2[:, :, 1], EPS, None, ALU.add).then_inc(s_var2, 1)
                eng.tensor_scalar(neg_mean2[:], mv2[:, :, 0], -1.0, None, ALU.mult).then_inc(s_mean2, 1)
                wait(s_var2, b + 1)
                eng.tensor_tensor(rstd2[:], var2[:], minus_half[:], ALU.pow).then_inc(s_rstd2, 1)
                wait(s_rstd2, b + 1)
                wait(s_mean2, b + 1)
                wait(s_ftr, b)
                for t in range(TT):
                    eng.tensor_scalar(f_hat[:, t, :], xy[:, b % XR, t * E:(t + 1) * E],
                                      neg_mean2[:, t:t + 1], rstd2[:, t:t + 1], ALU.add, ALU.mult).then_inc(s_fhat, 1)

            early = None
            for kind, i in slots():
                if kind == "ffn":
                    i = early = i * GROUP + GROUP + LAG
                    if i + 2 < NB:
                        prepare(i + 2)
                        query_hat(i + 2)
                        key_hat(i + 2)
                    continue
                if 0 <= i - NORM_LAG < NB:
                    norm_2(i - NORM_LAG)
                if i + 2 < NB and i != early:
                    prepare(i + 2)
                    query_hat(i + 2)
                    key_hat(i + 2)
                if i + 2 < NB:
                    values(i + 2)

        @block.vector
        def _(eng):
            wait = Waits(eng)
            wait(s_pool0, 8)
            eng.tensor_copy(ident16[:], ident[:]).then_inc(s_vec0, 1)
            wait(s_mask, 16)
            eng.tensor_copy(mask_f[:], mask_u8[:]).then_inc(s_vec0, 1)

            def constants():
                wait(s_w, n_weights)
                eng.memset(w4rep[:], 0.0).then_inc(s_vec0, 1)
                eng.tensor_scalar(half_b4[:], scal[:, 2:3], 0.5, None, ALU.mult).then_inc(s_vec0, 1)
                eng.tensor_scalar(half_gb3[:], scal[:, 3:4], 0.5, None, ALU.mult).then_inc(s_vec0, 1)
                eng.tensor_scalar(sign_ar[:], scal[:, 4:5], sign[:, 0:1], None, ALU.mult).then_inc(s_vec0, 1)
                eng.tensor_scalar(cs_base[:], sign[:], 0.1, None, ALU.mult).then_inc(s_vec0, 1)
                eng.tensor_scalar(u_scale[:], scal[:, 0:1], 1.0 / (Q_SCALE * K_SCALE * DH ** 0.5), None, ALU.mult) \
                   .then_inc(s_vec0, 1)
                eng.tensor_scalar(g3rep[0:G2, :], ones[0:G2, :], g3col[0:G2, 0:1], None, ALU.mult).then_inc(s_vec0, 1)
                wait(s_vec0, 9)
                eng.tensor_scalar(w4rep[0:M3, 0, :], ones[0:M3, :], w4col[0:M3, 0:1], None, ALU.mult).then_inc(s_vec0, 1)
                eng.tensor_scalar(w4rep[M3:P, 1, :], ones[M3:P, :], w4col[M3:P, 0:1], None, ALU.mult).then_inc(s_vec0, 1)
                eng.tensor_scalar(cs_tok[:], sign_ar[:], 0.3, None, ALU.mult).then_inc(s_vec0, 1)
                eng.tensor_scalar(cs_glob[:], sign_ar[:], 0.7, None, ALU.mult).then_inc(s_vec0, 1)
                wait(s_act0, 1)
                eng.tensor_scalar(shift[:], clip[:], -EXP_ROOM, 0.0, ALU.add, ALU.max).then_inc(s_vec0, 1)
                wait(s_pe0, 2)
                eng.tensor_copy(wo_t[:].rearrange("p k e -> p (k e)"), banks(X_BANK)).then_inc(s_vec0, 1)
                wait(s_vec0, 15)
                eng.tensor_scalar(exp_bias[:], banks(TR_BANK)[0:KEYS, 0:NB], MASKED, shift[0:KEYS, 0:1],
                                  ALU.mult, ALU.subtract).then_inc(s_vec0, 1)

            def stats(b):
                wait(s_ldx[b % NLOAD], 16 * (b // NLOAD + 1))
                for t in range(TT):
                    wait(s_mv, 2 * b)
                    eng.bn_stats(stats1[:, t, :], xy[:, b % XR, t * E:(t + 1) * E]).then_inc(s_stats, 1)
                if b >= 2:
                    wait(s_rstd, b - 1)
                    wait(s_mean, b - 1)
                for t in range(TT):
                    wait(s_stats, 2 * b + t + 1)
                    eng.bn_aggr(mv1[:, b % 2, t, :], stats1[:, t, :]).then_inc(s_mv, 1)

            def key_max(b):
                wait(s_ldc[b % NLOAD], 16 * (b // NLOAD + 1))
                wait(s_kamax, b)
                eng.tensor_reduce(k_max[:], cbuf[:, b % NLOAD, :], AX.X, ALU.max, apply_absolute_value=True) \
                   .then_inc(s_kmax, 1)

            def key_scale(b):
                wait(s_kmax, b + 1)
                wait(s_tsc, b)
                eng.tensor_scalar(k_amax[:], k_max[:], TINY, None, ALU.max).then_inc(s_kamax, 1)

            def key_inverse(b):
                wait(s_kamax, b + 1)
                wait(s_khat, b)
                eng.reciprocal(k_inv[:], k_amax[:]).then_inc(s_kinv, 1)
                if b >= 4:
                    wait(s_tanh, NG * (b - 3))
                eng.tensor_scalar(t_scale[:, b % 4, :], k_amax[:], u_scale[0:KEYS, 0:1], 1.0, ALU.mult, ALU.mult) \
                   .then_inc(s_tsc, 1)

            HEAD = 4 * 2 * DH

            def kz_heads(b, part):
                z = kz[:, b % 2, 0, part, 0, :]
                return bass.AP(z.tensor, z.offset, [list(z.ap[0]), [2 * HEAD, PAIRS], [HEAD + DH, 2], [1, DH]])

            def key_high(b):
                wait(s_khat, b + 1)
                if b >= 2:
                    wait(s_ktr, 2 * (b - 1))
                eng.tensor_copy(kz_heads(b, 0), k_hat[:].rearrange("k (p j d) -> k p j d", j=2, d=DH)) \
                   .then_inc(s_khi, 1)

            def key_low(b):
                wait(s_khi, b + 1)
                eng.tensor_tensor(kz_heads(b, 1), k_hat[:].rearrange("k (p j d) -> k p j d", j=2, d=DH),
                                  kz_heads(b, 0), ALU.subtract).then_inc(s_klo, 1)

            def key_twice(b):
                wait(s_klo, b + 1)
                eng.tensor_copy(kz[:, b % 2, :, :, 1, :], kz[:, b % 2, :, :, 0, :]).then_inc(s_kz, 1)

            q_pairs = q_hat[:].rearrange("p t (a d) -> p (t a) d", d=2 * DH)

            def q_part(b, part):
                return q_hl[:, b % 2].rearrange("p t a r h d -> p (t a) r h d")[:, :, 0, part, :]

            def query_high(b):
                wait(s_qhat, 2 * (b + 1))
                if b >= 2:
                    wait(s_qtr, 2 * (b - 1))
                eng.tensor_scalar(q_part(b, 0), q_pairs, Q_SCALE, None, ALU.mult).then_inc(s_qhi, 1)

            def query_low(b):
                wait(s_qhi, b + 1)
                eng.scalar_tensor_tensor(q_part(b, 1), q_pairs, Q_SCALE, q_part(b, 0),
                                         ALU.mult, ALU.subtract).then_inc(s_qlo, 1)

            def query_twice(b):
                wait(s_qlo, b + 1)
                both = q_hl[:, b % 2].rearrange("p t a r h d -> p (t a) r (h d)")
                eng.tensor_copy(both[:, :, 1, :], both[:, :, 0, :]).then_inc(s_qhl, 1)

            def q_stack(b, t):
                wait(s_qtr, 2 * b + t + 1)
                if b >= 2:
                    wait(s_score, NG * (b - 1))
                eng.tensor_copy(q_st[:, b % 2, :, t * P:(t + 1) * P],
                                banks(TR_BANK).bitcast(F16).rearrange("p (a q) -> p a q", q=P)).then_inc(s_qst, 1)

            def k_stack(b, n):
                wait(s_ktr, 2 * b + n + 1)
                if b >= 2:
                    wait(s_score, NG * (b - 1))
                eng.tensor_copy(k_st[:, b % 2, n * PAIRS:(n + 1) * PAIRS, :],
                                banks(TR_BANK).bitcast(F16)[:, 0:PAIRS * KEYS].rearrange("p (a q) -> p a q", q=KEYS)) \
                   .then_inc(s_kst, 1)

            def divide(b):
                for t in range(TT):
                    heads = banks(PV_BANKS[t]).rearrange("p (h s) -> p h s", s=SLOT)
                    wait(s_otr, 2 * b + t + 1)
                    wait(s_otok, 2 * (b - 1) + t + 1)
                    eng.reciprocal(inv_sum[:, t, :], heads[:, :, DH]).then_inc(s_inv, 1)
                for t in range(TT):
                    heads = banks(PV_BANKS[t]).rearrange("p (h s) -> p h s", s=SLOT)
                    wait(s_inv, 2 * b + t + 1)
                    wait(s_oftr, b)
                    eng.tensor_tensor(o_tok[:, t, :].rearrange("p (h d) -> p h d", d=DH), heads[:, :, 0:DH],
                                      inv_sum[:, t, :].unsqueeze(2).to_broadcast([P, H, DH]), ALU.mult) \
                       .then_inc(s_otok, 1)

            def attn_features(b):
                wait(s_oftr, b + 1)
                wait(s_proj, b)
                eng.tensor_copy(of_t[:].rearrange("p k q -> p (k q)"), banks(X_BANK)).then_inc(s_oft, 1)

            def residual(b):
                wait(s_proj, b + 1)
                eng.tensor_tensor(xy[:, b % XR, :], xy[:, b % XR, :], banks(X_BANK), ALU.add).then_inc(s_y, 1)

            def stats_2(b):
                wait(s_y, b + 1)
                wait(s_mv2, 2 * b)
                for t in range(TT):
                    eng.bn_stats(stats2[:, t, :], xy[:, b % XR, t * E:(t + 1) * E]).then_inc(s_stats2, 1)
                wait(s_rstd2, b)
                wait(s_mean2, b)
                for t in range(TT):
                    wait(s_stats2, 2 * b + t + 1)
                    eng.bn_aggr(mv2[:, t, :], stats2[:, t, :]).then_inc(s_mv2, 1)

            def update(n, chunk, half):
                turn = 2 * n + half
                wait(s_coup, (turn + 1) * CB // 2)
                if turn >= 2:
                    wait(s_upd, EK * (turn - 1))
                tok = slice(chunk * CT + half * HALF, chunk * CT + (half + 1) * HALF)
                here = slice(half * HALF, (half + 1) * HALF)
                for k in range(EK):
                    eng.tensor_tensor(move[:, k, here], f_t[:, 1 - k, tok], coup[:, chunk, here], ALU.mult) \
                       .then_inc(s_move, 1)
                for k in range(EK):
                    wait(s_move, EK * (turn + 1))
                    eng.tensor_tensor(f_t[:, k, tok], f_t[:, k, tok], move[:, k, here],
                                      (ALU.add, ALU.subtract)[k]).then_inc(s_upd, 1)

            def results(b):
                wait(s_back, b + 1)
                eng.tensor_tensor(xy[:, b % XR, :], xy[:, b % XR, :], banks(PV_BANKS[b % 2]), ALU.add) \
                   .then_inc(s_res, 1)

            def second_norm(b):
                residual(b)
                stats_2(b)

            late, rest, early = [], None, None
            for kind, i in slots():
                if kind == "attention":
                    new, nxt, old, last = i + 2, i + 1, i - 2, i - NORM_LAG
                    fresh, ahead, past = new < NB and i != early, 0 <= nxt < NB, 0 <= old < NB
                    if 0 <= last < NB and i != early:
                        second_norm(last)
                    for b in late[:2]:
                        results(b)
                    late = late[2:]
                    if ahead:
                        q_stack(nxt, 0)
                    if past:
                        divide(old)
                    if fresh:
                        stats(new)
                    if i == -2:
                        constants()
                    if ahead:
                        q_stack(nxt, 1)
                    if rest is not None:
                        update(rest, 1, 1)
                        rest = None
                    if fresh:
                        key_max(new)
                        key_scale(new)
                        key_inverse(new)
                    if ahead:
                        k_stack(nxt, 0)
                    if past:
                        attn_features(old)
                    if fresh:
                        query_high(new)
                        key_high(new)
                    if ahead:
                        k_stack(nxt, 1)
                    if fresh:
                        query_low(new)
                        key_low(new)
                        query_twice(new)
                        key_twice(new)
                else:
                    early = i * GROUP + GROUP + LAG
                    new = early + 2
                    if early - NORM_LAG < NB:
                        second_norm(early - NORM_LAG)
                    if new < NB:
                        stats(new)
                        key_max(new)
                        key_scale(new)
                        key_inverse(new)
                        query_high(new)
                        key_high(new)
                        query_low(new)
                        key_low(new)
                        query_twice(new)
                        key_twice(new)
                    for cyc, na, nb in passes(i):
                        if cyc == 0:
                            wait(s_gact, 3 * (i + 1))
                            if i:
                                wait(s_coup, i * CYCLES * GROUP)
                            eng.tensor_scalar(cs_batch[:], gth[:], cs_glob[:, 0:1], cs_base[:, 0:1],
                                              ALU.mult, ALU.add).then_inc(s_gcs, 1)
                        update(na, 0, 0)
                        update(na, 0, 1)
                        update(nb, 1, 0)
                        if cyc < CYCLES - 1:
                            update(nb, 1, 1)
                    rest = nb
                    late = list(range(i * GROUP, (i + 1) * GROUP))
            for b in late:
                results(b)

        @block.scalar
        def _(eng):
            wait = Waits(eng)
            wait(s_w, n_weights)
            eng.activation(clip[:], scal[:, 1:2], ACT.Exp).then_inc(s_act0, 1)

            def tanh(b, n):
                wait(s_score, NG * b + n + 1)
                wait(s_tsc, b + 1)
                if b >= 2:
                    wait(s_pv, 2 * (b - 2) + n // 2 + 1)
                first = SCORE_BANKS[n % 2][0]
                eng.activation(probs[:, b % 2, n * HG:(n + 1) * HG, :].rearrange("k h q -> k (h q)"),
                               banks(first, 2)[0:KEYS, :], ACT.Tanh, scale=t_scale[:, b % 4, :]).then_inc(s_tanh, 1)

            def exp(b, n):
                wait(s_tanh, NG * b + 2 * n + 2)
                p = probs[:, b % 2, 2 * n * HG:2 * (n + 1) * HG, :].rearrange("k h q -> k (h q)")
                eng.activation(p, p, ACT.Exp, scale=clip[0:KEYS, 0:1], bias=exp_bias[:, b:b + 1]).then_inc(s_exp, 1)

            def attn_out(b, n):
                wait(s_pv, 2 * b + n + 1)
                if b >= 2:
                    wait(s_otr, 2 * (b - 1))
                eng.activation(o_t[:, b % 2, 2 * n:2 * n + 2, :].rearrange("p c q -> p (c q)"),
                               banks(PV_BANKS[n]), ACT.Copy).then_inc(s_ot, 1)

            def features(b):
                wait(s_ftr, b + 1)
                if b >= GROUP:
                    g = b // GROUP
                    wait(s_back, b - GROUP + 1)
                    wait(s_glob, 3 * g)
                at = b % GROUP
                for k in range(EK):
                    eng.activation(f_t[:, k, at * S:(at + 1) * S], banks(X_BANK)[:, k * S:(k + 1) * S],
                                   ACT.Identity, accum_out=f_sum[:, k, at:at + 1]).then_inc(s_ft, 1)

            def gelu1(n, chunk):
                if n >= 2:
                    wait(s_l2, 2 * (n - 1))
                for m in range(EK):
                    wait(s_l1, 2 * n + m + 1)
                    eng.activation(h1[:, chunk, m, :], banks(SCORE_BANKS[m][0], 2), ACT.Gelu, bias=b1[:, m:m + 1]) \
                       .then_inc(s_h1, 1)

            def gelu2(n, chunk, half):
                wait(s_l2, 2 * n + half + 1)
                if n >= 2:
                    wait(s_l3, n - 1)
                eng.activation(h2[:, chunk, half * HALF:(half + 1) * HALF], banks(PV_BANKS[half]), ACT.Gelu,
                               bias=b2[:, 0:1]).then_inc(s_h2, 1)

            def gelu3(n, chunk):
                wait(s_l3, n + 1)
                if n >= 2:
                    wait(s_l4, 2 * (n - 1))
                eng.activation(h3[:, chunk, :], banks(L3_BANKS[chunk]), ACT.Gelu, bias=b3[:, 0:1]).then_inc(s_h3, 1)

            def coupling(g, n, chunk, half):
                wait(s_l4, 2 * n + half + 1)
                if n >= 2:
                    wait(s_move, EK * (2 * (n - 2) + half + 1))
                eng.activation(coup[:, chunk, half * HALF:(half + 1) * HALF], banks(L4_BANKS[half]), ACT.Tanh,
                               scale=0.5, bias=half_b4[:, 0:1]).then_inc(s_th, 1)
                wait(s_gcs, g + 1)
                wait(s_th, 2 * n + half + 1)
                for b in range(half * CB // 2, (half + 1) * CB // 2):
                    c = coup[:, chunk, b * S:(b + 1) * S]
                    eng.activation(c, c, ACT.Identity, scale=cs_tok[:, 0:1],
                                   bias=cs_batch[:, chunk * CB + b:chunk * CB + b + 1]).then_inc(s_coup, 1)

            wait(s_vec0, 16)
            for kind, i in slots():
                if kind == "attention":
                    on, past = 0 <= i < NB, 0 <= i - 1 < NB
                    if on:
                        tanh(i, 0)
                        tanh(i, 1)
                        exp(i, 0)
                    if 0 <= i - LAG < NB:
                        features(i - LAG)
                    if past:
                        attn_out(i - 1, 1)
                    if on:
                        tanh(i, 2)
                        tanh(i, 3)
                        exp(i, 1)
                        attn_out(i, 0)
                else:
                    glob = banks(TR_BANK)
                    for cyc, na, nb in passes(i):
                        gelu1(na, 0)
                        if cyc == 0:
                            wait(s_glob, 3 * i + 1)
                            eng.activation(gh1[:], glob[:, 0:GROUP], ACT.Gelu, bias=gb1[:, 0:1], scale=1.0 / S) \
                               .then_inc(s_gact, 1)
                        gelu1(nb, 1)
                        if cyc == 0:
                            wait(s_glob, 3 * i + 2)
                            eng.activation(gh2[0:G2, :], glob[0:G2, GROUP:2 * GROUP], ACT.Gelu, bias=gb2[0:G2, 0:1]) \
                               .then_inc(s_gact, 1)
                        gelu2(na, 0, 0)
                        gelu2(na, 0, 1)
                        if cyc == 0:
                            wait(s_glob, 3 * i + 3)
                            if i:
                                wait(s_gcs, i)
                            eng.activation(gth[:], glob[:, 2 * GROUP:3 * GROUP], ACT.Tanh, scale=0.5,
                                           bias=half_gb3[:, 0:1]).then_inc(s_gact, 1)
                        gelu2(nb, 1, 0)
                        gelu3(na, 0)
                        gelu2(nb, 1, 1)
                        coupling(i, na, 0, 0)
                        coupling(i, na, 0, 1)
                        gelu3(nb, 1)
                        coupling(i, nb, 1, 0)
                        coupling(i, nb, 1, 1)

        @block.tensor
        def _(eng):
            wait = Waits(eng)
            reader = {}

            def claim(*which):
                for bank in which:
                    if bank in reader:
                        wait(*reader[bank])

            def read_by(s, n, *which):
                for bank in which:
                    reader[bank] = (s, n)

            wait(s_pool0, 4)
            wait(s_w, n_weights)
            for k in range(EK):
                for m in range(EK):
                    last = eng.transpose(banks(X_BANK)[:, k * E + m * P:k * E + (m + 1) * P],
                                         wo_in[:, m, k * P:(k + 1) * P], ident[:])
            last.then_inc(s_pe0, 1)
            wait(s_vec0, 2)
            eng.transpose(banks(TR_BANK)[0:KEYS, 0:NB], mask_f[:], ident[0:NB, 0:NB]).then_inc(s_pe0, 1)
            read_by(s_vec0, 16, X_BANK, TR_BANK)

            def query_stack(b, t):
                wait(s_qhl, b + 1)
                claim(TR_BANK)
                dst = banks(TR_BANK).bitcast(F16)
                for pair in range(PAIRS):
                    last = eng.transpose(dst[:, pair * P:(pair + 1) * P],
                                         q_hl[:, b % 2, t, pair].rearrange("p r h d -> p (r h d)"), ident16[:])
                last.then_inc(s_qtr, 1)
                read_by(s_qst, 2 * b + t + 1, TR_BANK)

            def key_stack(b, n):
                wait(s_kz, b + 1)
                claim(TR_BANK)
                dst = banks(TR_BANK).bitcast(F16)
                for j in range(PAIRS):
                    last = eng.transpose(dst[:, j * KEYS:(j + 1) * KEYS],
                                         kz[:, b % 2, n * PAIRS + j].rearrange("k h r d -> k (h r d)"),
                                         ident16[0:KEYS, 0:KEYS])
                last.then_inc(s_ktr, 1)
                read_by(s_kst, 2 * b + n + 1, TR_BANK)

            def scores(b, n):
                wait(s_qst, 2 * (b + 1))
                wait(s_kst, 2 * b + n // 2 + 1)
                pair_of_banks = SCORE_BANKS[n % 2]
                claim(*pair_of_banks)
                for j in range(HG):
                    h = n * HG + j
                    last = eng.matmul(banks(pair_of_banks[0], 2)[0:KEYS, j * S:(j + 1) * S],
                                      k_st[:, b % 2, h, :], q_st[:, b % 2, h // 2, :], start=True, stop=True)
                last.then_inc(s_score, 1)
                read_by(s_tanh, NG * b + n + 1, *pair_of_banks)

            def weighted_values(b, n):
                wait(s_exp, 2 * b + n + 1)
                wait(s_va, b + 1)
                claim(PV_BANKS[n])
                for c in (2 * n, 2 * n + 1):
                    for j in range(HG):
                        h = c * HG + j
                        last = eng.matmul(banks(PV_BANKS[n])[j * SLOT:(j + 1) * SLOT, (c % 2) * S:(c % 2 + 1) * S],
                                          va[:, b % 3, h, :], probs[:, b % 2, h, :], start=True, stop=True,
                                          tile_position=(0, j * SLOT))
                last.then_inc(s_pv, 1)
                read_by(s_ot, 2 * b + n + 1, PV_BANKS[n])

            def attn_to_tokens(b):
                wait(s_ot, 2 * (b + 1))
                for t in range(TT):
                    claim(PV_BANKS[t])
                    for c in range(NG):
                        last = eng.transpose(banks(PV_BANKS[t])[:, c * P:(c + 1) * P],
                                             o_t[:, b % 2, c, t * P:(t + 1) * P], ident[:])
                    last.then_inc(s_otr, 1)
                    read_by(s_otok, 2 * b + t + 1, PV_BANKS[t])

            def attn_to_features(b):
                wait(s_otok, 2 * (b + 1))
                claim(X_BANK)
                for k in range(EK):
                    for t in range(TT):
                        last = eng.transpose(banks(X_BANK)[:, k * S + t * P:k * S + (t + 1) * P],
                                             o_tok[:, t, k * P:(k + 1) * P], ident[:])
                last.then_inc(s_oftr, 1)
                read_by(s_oft, b + 1, X_BANK)

            def project(b):
                wait(s_oft, b + 1)
                claim(X_BANK)
                for t in range(TT):
                    for k in range(EK):
                        last = eng.matmul(banks(X_BANK)[:, t * E:(t + 1) * E], of_t[:, k, t * P:(t + 1) * P],
                                          wo_t[:, k, :], start=(k == 0), stop=(k == EK - 1))
                last.then_inc(s_proj, 1)
                read_by(s_y, b + 1, X_BANK)

            def norm_to_features(b):
                wait(s_fhat, 2 * (b + 1))
                claim(X_BANK)
                for k in range(EK):
                    for t in range(TT):
                        last = eng.transpose(banks(X_BANK)[:, k * S + t * P:k * S + (t + 1) * P],
                                             f_hat[:, t, k * P:(k + 1) * P], ident[:])
                last.then_inc(s_ftr, 1)
                read_by(s_ft, 2 * (b + 1), X_BANK)

            def layer1(g, n, chunk):
                if n < 2 * CYCLES * g + 2:
                    wait(s_ft, 2 * (g * GROUP + (chunk + 1) * CB))
                for m in range(EK):
                    claim(*SCORE_BANKS[m])
                for half in range(2):
                    if n >= 2 * CYCLES * g + 2:
                        wait(s_upd, EK * (2 * (n - 2) + half + 1))
                    tok = chunk * CT + half * HALF
                    for m in range(EK):
                        for k in range(EK):
                            last = eng.matmul(banks(SCORE_BANKS[m][half]), w1[:, k, m * P:(m + 1) * P],
                                              f_t[:, k, tok:tok + HALF], start=(k == 0), stop=(k == EK - 1))
                        if half:
                            last.then_inc(s_l1, 1)
                for m in range(EK):
                    read_by(s_h1, 2 * n + m + 1, *SCORE_BANKS[m])

            def layer2(n, chunk, half):
                wait(s_h1, 2 * (n + 1))
                claim(PV_BANKS[half])
                for k in range(EK):
                    last = eng.matmul(banks(PV_BANKS[half]), w2[:, k, :], h1[:, chunk, k, half * HALF:(half + 1) * HALF],
                                      start=(k == 0), stop=(k == EK - 1))
                last.then_inc(s_l2, 1)
                read_by(s_h2, 2 * n + half + 1, PV_BANKS[half])

            def layer3(n, chunk):
                wait(s_h2, 2 * (n + 1))
                claim(L3_BANKS[chunk])
                for half in range(2):
                    last = eng.matmul(banks(L3_BANKS[chunk])[half * M3:(half + 1) * M3, :], w3[:],
                                      h2[:, chunk, half * HALF:(half + 1) * HALF], start=True, stop=True,
                                      tile_position=(0, half * M3))
                last.then_inc(s_l3, 1)
                read_by(s_h3, n + 1, L3_BANKS[chunk])

            def layer4(n, chunk):
                wait(s_h3, n + 1)
                for half in range(2):
                    claim(L4_BANKS[half])
                    eng.matmul(banks(L4_BANKS[half]), w4rep[:, half, :], h3[:, chunk, :], start=True, stop=True) \
                       .then_inc(s_l4, 1)
                    read_by(s_th, 2 * n + half + 1, L4_BANKS[half])

            def global_net(g, layer):
                dst = banks(TR_BANK)
                if layer == 0:
                    wait(s_ft, 2 * (g + 1) * GROUP)
                    claim(TR_BANK)
                    for k in range(EK):
                        last = eng.matmul(dst[:, 0:GROUP], g1[:, k, :], f_sum[:, k, :], start=(k == 0), stop=(k == EK - 1))
                else:
                    wait(s_gact, 3 * g + layer)
                    if layer == 1:
                        last = eng.matmul(dst[0:G2, GROUP:2 * GROUP], g2[:], gh1[:], start=True, stop=True)
                    else:
                        last = eng.matmul(dst[:, 2 * GROUP:3 * GROUP], g3rep[0:G2, :], gh2[0:G2, :],
                                          start=True, stop=True)
                last.then_inc(s_glob, 1)
                read_by(s_gact, 3 * g + layer + 1, TR_BANK)

            def to_tokens(b, n):
                wait(s_upd, EK * (2 * n + (b % CB) // (CB // 2) + 1))
                bank, at = PV_BANKS[b % 2], b % GROUP
                claim(bank)
                for t in range(TT):
                    for k in range(EK):
                        last = eng.transpose(banks(bank)[:, t * E + k * P:t * E + (k + 1) * P],
                                             f_t[:, k, at * S + t * P:at * S + (t + 1) * P], ident[:])
                last.then_inc(s_back, 1)
                read_by(s_res, b + 1, bank)

            late = []
            for kind, i in slots():
                if kind == "attention":
                    nxt, done, old = i + 1, i - 1, i - 2
                    on, ahead, past, older = 0 <= i < NB, 0 <= nxt < NB, 0 <= done < NB, 0 <= old < NB
                    if on:
                        scores(i, 0)
                        scores(i, 1)
                    for b, n in late[:2]:
                        to_tokens(b, n)
                    late = late[2:]
                    if ahead:
                        query_stack(nxt, 0)
                    if 0 <= i - LAG < NB:
                        norm_to_features(i - LAG)
                    if older:
                        attn_to_tokens(old)
                    if ahead:
                        query_stack(nxt, 1)
                    if past:
                        weighted_values(done, 1)
                    if on:
                        scores(i, 2)
                        scores(i, 3)
                    if ahead:
                        key_stack(nxt, 0)
                    if older:
                        attn_to_features(old)
                    if on:
                        weighted_values(i, 0)
                    if ahead:
                        key_stack(nxt, 1)
                    if older:
                        project(old)
                else:
                    for cyc, na, nb in passes(i):
                        layer1(i, na, 0)
                        if cyc == 0:
                            global_net(i, 0)
                        layer1(i, nb, 1)
                        if cyc == 0:
                            global_net(i, 1)
                        layer2(na, 0, 0)
                        layer2(na, 0, 1)
                        if cyc == 0:
                            global_net(i, 2)
                        layer2(nb, 1, 0)
                        layer3(na, 0)
                        layer2(nb, 1, 1)
                        layer4(na, 0)
                        layer3(nb, 1)
                        layer4(nb, 1)
                    first = i * GROUP
                    late = [(first + k, na if k < CB else nb) for k in range(GROUP)]
            for b, n in late:
                to_tokens(b, n)


_INS = ['x', 'ctx_1024', 'mask_Bx1xS2_bk0', 'L0_xattn_W_out', 'L0_xattn_scale', 'L0_xattn_log_C',
        'L0_ffn_cn_w1', 'L0_ffn_cn_b1', 'L0_ffn_cn_w2', 'L0_ffn_cn_b2', 'L0_ffn_cn_w3', 'L0_ffn_cn_b3',
        'L0_ffn_cn_w4', 'L0_ffn_cn_b4', 'L0_ffn_gc_w1', 'L0_ffn_gc_b1', 'L0_ffn_gc_w2', 'L0_ffn_gc_b2',
        'L0_ffn_gc_w3', 'L0_ffn_gc_b3', 'L0_ffn_adaptive_range']


def kernel(**inputs):
    import numpy as _np
    import concourse.bacc as _bacc
    from concourse import mybir as _mybir
    from concourse.bass_utils import run_bass_kernel_spmd as _run

    nc = _bacc.Bacc("TRN2", target_bir_lowering=False, num_devices=1)
    arrays, args = {}, []
    for name in _INS:
        a = _np.ascontiguousarray(inputs[name])
        a = a.reshape(a.shape or (1,))
        arrays[f"in_{name}_dram"] = a
        args.append(nc.dram_tensor(f"in_{name}_dram", a.shape, _mybir.dt.from_np(a.dtype), kind="ExternalInput").ap())
    shape = tuple(inputs['x'].shape)
    args.append(nc.dram_tensor("out_0_dram", shape, _mybir.dt.float32, kind="ExternalOutput").ap())
    xattn_ffn_kernel(nc, *args)
    r = _run(nc, [arrays], core_ids=[0])
    return r.results[0]["out_0_dram"]
```

```python
from contextlib import ExitStack

import concourse.bass as bass
from concourse import mybir

ALU = mybir.AluOpType
ACT = mybir.ActivationFunctionType
AX = mybir.AxisListType
F32 = mybir.dt.float32
F16 = mybir.dt.float16
U8 = mybir.dt.uint8

P = 128
EPS = 1e-5
MASKED = -1e30
EXP_ROOM = 64.0
Q_SCALE = 256.0
F_SCALE = 256.0
W_SCALE = 256.0
K_SCALE = 256.0
TINY = 1e-30


class Waits:

    def __init__(self, eng):
        self.eng, self.seen = eng, {}

    def __call__(self, sem, n):
        if n > self.seen.get(sem.name, 0):
            self.eng.wait_ge(sem, n)
            self.seen[sem.name] = n


def xattn_ffn_kernel(nc, x, ctx, mask, W_out, scale, log_C,
                     cn_w1, cn_b1, cn_w2, cn_b2, cn_w3, cn_b3, cn_w4, cn_b4,
                     gc_w1, gc_b1, gc_w2, gc_b2, gc_w3, gc_b3, adaptive_range, out):
    NB, S, E = x.shape
    KEYS = ctx.shape[1]
    H, DH = 16, 16
    TT = S // P
    EK = E // P
    PAIRS = H // 2
    HG = 4
    NG = H // HG
    SLOT = 2 * DH
    M2, M3 = cn_w2.shape[1], cn_w3.shape[1]
    G1, G2 = gc_w1.shape[1], gc_w2.shape[1]
    GROUP = 8
    CB = 2
    CT = CB * S
    CHUNKS = GROUP // CB
    CYCLES = 3
    PASSES = CYCLES * CHUNKS
    UPDATES = (CYCLES - 1) * CHUNKS
    NORM_LAG = 3
    LAG = 4
    XR = 16
    NLOAD = 4
    BANK = 512
    NGROUPS = NB // GROUP

    with ExitStack() as stack:
        def sb(name, shape, dt=F32):
            return stack.enter_context(nc.sbuf_tensor(name, shape, dt))

        def sem(name):
            return stack.enter_context(nc.semaphore(name))

        ident = sb("ident", [P, P])
        ident16 = sb("ident16", [P, P], F16)
        ones = sb("ones", [P, P])
        wo_t = sb("wo_t", [P, EK, E])
        w1_hl = sb("w1_hl", [P, 2, EK, E], F16)
        w1t_hl = sb("w1t_hl", [P, 2, EK, E], F16)
        w_max = sb("w_max", [P, 1])
        w_row = sb("w_row", [1, 1])
        w_inv = sb("w_inv", [P, 1])
        uv_scale = sb("uv_scale", [P, 1])
        w2 = sb("w2", [P, EK, M2])
        w3 = sb("w3", [P, M3])
        w4col = sb("w4col", [P, 1])
        w4rep = sb("w4rep", [P, 2, P])
        g1 = sb("g1", [P, EK, G1])
        g2 = sb("g2", [P, G2])
        g3col = sb("g3col", [P, 1])
        g3rep = sb("g3rep", [P, P])
        b1 = sb("b1", [P, EK])
        b2 = sb("b2", [P, 1])
        b3 = sb("b3", [P, 1])
        gb1 = sb("gb1", [P, 1])
        gb2 = sb("gb2", [P, 1])
        scal = sb("scal", [P, 8])
        half_b4 = sb("half_b4", [P, 1])
        half_gb3 = sb("half_gb3", [P, 1])
        sign = sb("sign", [P, 1])
        c_tok = sb("c_tok", [P, 1])
        c_glob = sb("c_glob", [P, 1])
        neg_sign = sb("neg_sign", [P, 1])
        clip = sb("clip", [P, 1])
        shift = sb("shift", [P, 1])
        u_scale = sb("u_scale", [P, 1])
        mask_u8 = sb("mask_u8", [NB, KEYS], U8)
        mask_f = sb("mask_f", [NB, KEYS])
        exp_bias = sb("exp_bias", [KEYS, NB])

        xy = sb("xy", [P, XR, TT * E])
        cbuf = sb("cbuf", [KEYS, NLOAD, E])
        va = sb("va", [KEYS, 3, H, SLOT])
        stats1 = sb("stats1", [P, TT, 6])
        mv1 = sb("mv1", [P, 2, TT, 2])
        rstd1 = sb("rstd1", [P, 2, TT])
        var1 = sb("var1", [P, TT])
        var2 = sb("var2", [P, TT])
        neg_mean1 = sb("neg_mean1", [P, TT])
        neg_mean2 = sb("neg_mean2", [P, XR, TT])
        minus_half = sb("minus_half", [P, TT])
        q_hat = sb("q_hat", [P, TT, E])
        q_hl = sb("q_hl", [P, 2, TT, PAIRS, 2, 2, 2 * DH], F16)
        k_max = sb("k_max", [KEYS, 1])
        k_amax = sb("k_amax", [KEYS, 1])
        k_inv = sb("k_inv", [KEYS, 1])
        t_scale = sb("t_scale", [KEYS, 4, 1])
        k_hat = sb("k_hat", [KEYS, E])
        kz = sb("kz", [KEYS, 2, H, 2, 2, 2 * DH], F16)
        q_st = sb("q_st", [P, 2, PAIRS, S], F16)
        k_st = sb("k_st", [P, 2, H, KEYS], F16)
        probs = sb("probs", [KEYS, 2, H, S])
        o_t = sb("o_t", [P, 2, NG, S])
        inv_sum = sb("inv_sum", [P, TT, H])
        o_tok = sb("o_tok", [P, TT, E])
        of_t = sb("of_t", [P, EK, S])
        stats2 = sb("stats2", [P, TT, 6])
        mv2 = sb("mv2", [P, TT, 2])
        rstd2 = sb("rstd2", [P, XR, TT])
        f_hat = sb("f_hat", [P, TT, E])

        f_t = sb("f_t", [P, EK, GROUP * S])
        v_t = sb("v_t", [P, EK, GROUP * S])
        f_sum = sb("f_sum", [P, EK, GROUP])
        h1 = sb("h1", [P, 2, EK, CT])
        h2 = sb("h2", [P, 2, CT])
        h3 = sb("h3", [P, 2, S])
        coup = sb("coup", [P, 2, CT])
        move_u = sb("move_u", [P, EK, CT])
        move_v = sb("move_v", [P, EK, CT])
        w1, w1_twist, wo_in = move_u[:, :, 0:E], move_u[:, :, E:2 * E], move_v[:, :, 0:E]
        f_hl = sb("f_hl", [P, 2, 2, EK, CT], F16)
        gh1 = sb("gh1", [P, GROUP])
        gh2 = sb("gh2", [P, GROUP])
        gth = sb("gth", [P, GROUP])
        c_batch = sb("c_batch", [P, GROUP])
        GT = TT * GROUP
        tok_th = sb("tok_th", [P, CYCLES, GT])
        tok_c = sb("tok_c", [P, CYCLES, GT])
        c12 = sb("c12", [P, GT])
        co_a2 = sb("co_a2", [P, GT])
        co_b2 = sb("co_b2", [P, GT])
        c3b2 = sb("c3b2", [P, GT])
        c3a2 = sb("c3a2", [P, GT])
        co_a3 = sb("co_a3", [P, GT])
        co_b3 = sb("co_b3", [P, GT])
        a3_r = sb("a3_r", [P, GT])
        b3_r = sb("b3_r", [P, GT])
        x_fac = sb("x_fac", [P, GT])
        x_add = sb("x_add", [P, GT])
        twisted = sb("twisted", [P, 2, TT, E])

        ps = stack.enter_context(nc.psum_tensor("ps", [P, 8, BANK], F32))
        ps_flat = ps[:].rearrange("p b n -> p (b n)")
        SCORE_BANKS = ((0, 1), (2, 3))
        PV_BANKS = (4, 5)
        TR_BANK = 6
        X_BANK = 7
        U_BANKS, V_BANKS = (0, 1), (2, 3)
        L2_BANKS = (4, 5)
        L3_BANK = TR_BANK
        SMALL_AT = S
        TOKEN_AT = S + 32
        L4_BANK = 7

        def banks(first, n=1):
            return ps_flat[:, first * BANK:(first + n) * BANK]

        s_w = sem("s_w")
        s_mask = sem("s_mask")
        s_scal = sem("s_scal")
        s_ldx = [sem(f"s_ldx{n}") for n in range(NLOAD)]
        s_ldc = [sem(f"s_ldc{n}") for n in range(NLOAD)]
        s_st = [sem(f"s_st{n}") for n in range(XR)]
        s_pool0, s_vec0, s_act0, s_pe0 = sem("s_pool0"), sem("s_vec0"), sem("s_act0"), sem("s_pe0")
        s_va = sem("s_va")
        s_stats = sem("s_stats")
        s_mv = sem("s_mv")
        s_var, s_var2 = sem("s_var"), sem("s_var2")
        s_mean, s_mean2 = sem("s_mean"), sem("s_mean2")
        s_rstd = sem("s_rstd")
        s_qhat = sem("s_qhat")
        s_qhi = sem("s_qhi")
        s_qlo = sem("s_qlo")
        s_qhl, s_kz = sem("s_qhl"), sem("s_kz")
        s_kmax, s_kamax, s_kinv = sem("s_kmax"), sem("s_kamax"), sem("s_kinv")
        s_tsc = sem("s_tsc")
        s_khat, s_khi, s_klo = sem("s_khat"), sem("s_khi"), sem("s_klo")
        s_qtr, s_ktr = sem("s_qtr"), sem("s_ktr")
        s_qst, s_kst = sem("s_qst"), sem("s_kst")
        s_score = sem("s_score")
        s_tanh = sem("s_tanh")
        s_exp = sem("s_exp")
        s_pv = sem("s_pv")
        s_ot = sem("s_ot")
        s_otr = sem("s_otr")
        s_inv = sem("s_inv")
        s_otok = sem("s_otok")
        s_oftr = sem("s_oftr")
        s_oft = sem("s_oft")
        s_proj = sem("s_proj")
        s_y = sem("s_y")
        s_stats2, s_mv2, s_rstd2, s_fhat = sem("s_stats2"), sem("s_mv2"), sem("s_rstd2"), sem("s_fhat")
        s_ftr = sem("s_ftr")
        s_ft = sem("s_ft")
        s_l1 = sem("s_l1")
        s_fhi, s_flo = sem("s_fhi"), sem("s_flo")
        s_uv = sem("s_uv")
        s_h1 = sem("s_h1")
        s_l2, s_h2 = sem("s_l2"), sem("s_h2")
        s_l3, s_h3 = sem("s_l3"), sem("s_h3")
        s_l4, s_th = sem("s_l4"), sem("s_th")
        s_coup = sem("s_coup")
        s_mvu, s_upd = sem("s_mvu"), sem("s_upd")
        s_mvv, s_vupd = sem("s_mvv"), sem("s_vupd")
        s_ztok = sem("s_ztok")
        s_ttok = sem("s_ttok")
        s_coef = sem("s_coef")
        s_tw, s_fac = sem("s_tw"), sem("s_fac")
        s_glob, s_gact, s_gcs = sem("s_glob"), sem("s_gact"), sem("s_gcs")
        s_res = sem("s_res")
        COEFS = 13

        N_MASK, N_BIAS, N_MAX, N_WO, N_ROW, N_SPREAD, N_SPLIT = 2, 5, 10, 16, 17, 18, 27

        block = stack.enter_context(nc.Block())

        def col(ap):
            return ap.rearrange("(p a) -> p a", a=1)

        weight_loads = [
            (wo_in, W_out.rearrange("(k p) f -> p k f", p=P)),
            (w1, cn_w1.rearrange("(k p) f -> p k f", p=P)),
            (w2[:], cn_w2.rearrange("(k p) f -> p k f", p=P)),
            (w3[:], cn_w3),
            (w4col[0:M3, :], cn_w4), (w4col[M3:P, :], cn_w4),
            (g1[:], gc_w1.rearrange("(k p) f -> p k f", p=P)),
            (g2[:], gc_w2),
            (g3col[0:G2, :], gc_w3),
            (b1[:, 0:1], col(cn_b1[0:P])), (b1[:, 1:2], col(cn_b1[P:E])),
            (b2[:], col(cn_b2)),
            (b3[0:M3, :], col(cn_b3)), (b3[M3:P, :], col(cn_b3)),
            (gb1[:], col(gc_b1)),
            (gb2[0:G2, :], col(gc_b2)),
        ]
        scalar_loads = [(scal[:, n:n + 1], one.partition_broadcast(P))
                        for n, one in enumerate((scale, log_C, cn_b4, gc_b3, adaptive_range))]
        weight_loads += scalar_loads[2:]
        n_weights = 16 * len(weight_loads)

        def slots():
            for i in range(-2, NB + LAG):
                yield "attention", i
                done = i - LAG
                if done >= 0 and (done + 1) % GROUP == 0:
                    yield "ffn", done // GROUP

        def slot_of(p):
            return p // CHUNKS, p % CHUNKS

        @block.sync
        def _(eng):
            wait = Waits(eng)
            eng.dma_start(mask_u8[:], mask.rearrange("b a k -> b (a k)")).then_inc(s_mask, 16)
            for dst, src in scalar_loads[:2]:
                eng.dma_start(dst, src).then_inc(s_scal, 16)

            def load(b):
                if b >= XR:
                    wait(s_st[b % XR], 16 * (b // XR))
                if b >= NLOAD:
                    wait(s_stats, 2 * (b - NLOAD + 1))
                eng.dma_start(xy[:, b % XR, :], x[b].rearrange("(p t) e -> p (t e)", t=TT)) \
                   .then_inc(s_ldx[b % NLOAD], 16)
                if b >= NLOAD:
                    wait(s_khat, b - NLOAD + 1)
                    wait(s_va, b - NLOAD + 1)
                eng.dma_start(cbuf[:, b % NLOAD, :], ctx[b]).then_inc(s_ldc[b % NLOAD], 16)

            def store(b):
                wait(s_res, 4 * (b + 1))
                eng.dma_start(out[b].rearrange("(p t) e -> p (t e)", t=TT), xy[:, b % XR, :]) \
                   .then_inc(s_st[b % XR], 16)

            late = []
            for kind, i in slots():
                if kind != "attention":
                    late = list(range(i * GROUP, (i + 1) * GROUP))
                    continue
                for b in late[:1]:
                    store(b)
                late = late[1:]
                if i == -2:
                    load(0)
                    load(1)
                    load(2)
                    for dst, src in weight_loads:
                        eng.dma_start(dst, src).then_inc(s_w, 16)
                elif 0 <= i + 4 < NB and i >= -1:
                    load(i + 4)
            for b in late:
                store(b)
            for n in range(XR):
                eng.wait_ge(s_st[n], 16 * (NB // XR))

        @block.gpsimd
        def _(eng):
            wait = Waits(eng)
            eng.memset(ident[:], 0.0).then_inc(s_pool0, 1)
            eng.memset(sign[:], 1.0).then_inc(s_pool0, 1)
            eng.wait_ge(s_pool0, 2)
            eng.affine_select(out=ident[:], in_=ident[:], compare_op=ALU.not_equal, fill=1.0, base=0,
                              pattern=[[-1, P]], channel_multiplier=1).then_inc(s_pool0, 1)
            eng.affine_select(out=sign[:], in_=sign[:], compare_op=ALU.is_ge, fill=-1.0, base=P // 2 - 1,
                              pattern=[[0, 1]], channel_multiplier=-1).then_inc(s_pool0, 1)
            eng.memset(ones[:], 1.0).then_inc(s_pool0, 1)
            eng.memset(va[:], 1.0).then_inc(s_pool0, 1)
            eng.memset(kz[:], 0.0).then_inc(s_pool0, 1)
            eng.memset(minus_half[:], -0.5).then_inc(s_pool0, 1)
            wait(s_pool0, 8)

            def prepare(b):
                wait(s_mv, 2 * (b + 1))
                if b >= 2:
                    wait(s_qhat, 2 * (b - 1))
                wait(s_rstd, b)
                eng.tensor_scalar(var1[:], mv1[:, b % 2, :, 1], EPS, None, ALU.add).then_inc(s_var, 1)
                wait(s_qhat, 2 * b)
                eng.tensor_scalar(neg_mean1[:], mv1[:, b % 2, :, 0], -1.0, None, ALU.mult).then_inc(s_mean, 1)
                wait(s_var, b + 1)
                eng.tensor_tensor(rstd1[:, b % 2, :], var1[:], minus_half[:], ALU.pow).then_inc(s_rstd, 1)

            def values(b):
                wait(s_ldc[b % NLOAD], 16 * (b // NLOAD + 1))
                if b >= 3:
                    wait(s_pv, 2 * (b - 2))
                eng.tensor_scalar(va[:, b % 3, :, 0:DH], cbuf[:, b % NLOAD, :].rearrange("k (h d) -> k h d", d=DH),
                                  1.0, None, ALU.mult).then_inc(s_va, 1)

            def query_hat(b):
                wait(s_rstd, b + 1)
                wait(s_mean, b + 1)
                wait(s_qlo, b)
                for t in range(TT):
                    eng.tensor_scalar(q_hat[:, t, :], xy[:, b % XR, t * E:(t + 1) * E],
                                      neg_mean1[:, t:t + 1], rstd1[:, b % 2, t:t + 1],
                                      ALU.add, ALU.mult).then_inc(s_qhat, 1)

            def key_hat(b):
                wait(s_kinv, b + 1)
                wait(s_klo, b)
                eng.tensor_scalar(k_hat[:], cbuf[:, b % NLOAD, :], k_inv[:, 0:1], K_SCALE, ALU.mult, ALU.mult) \
                   .then_inc(s_khat, 1)

            def norm_2(b):
                wait(s_mv2, 2 * (b + 1))
                wait(s_rstd2, b)
                at = b % XR
                eng.tensor_scalar(var2[:], mv2[:, :, 1], EPS, None, ALU.add).then_inc(s_var2, 1)
                eng.tensor_scalar(neg_mean2[:, at, :], mv2[:, :, 0], -1.0, None, ALU.mult).then_inc(s_mean2, 1)
                wait(s_var2, b + 1)
                eng.tensor_tensor(rstd2[:, at, :], var2[:], minus_half[:], ALU.pow).then_inc(s_rstd2, 1)
                wait(s_rstd2, b + 1)
                wait(s_mean2, b + 1)
                wait(s_ftr, b)
                for t in range(TT):
                    eng.tensor_scalar(f_hat[:, t, :], xy[:, b % XR, t * E:(t + 1) * E],
                                      neg_mean2[:, at, t:t + 1], rstd2[:, at, t:t + 1],
                                      ALU.add, ALU.mult).then_inc(s_fhat, 1)

            def update_v(g, chunk):
                turn, number = UPDATES * g + chunk, CHUNKS * g + chunk
                tok = slice(chunk * CT, (chunk + 1) * CT)
                wait(s_uv, 2 * EK * (number + 1))
                wait(s_coup, CB * (turn + 1))
                wait(s_vupd, EK * number)
                for m in range(EK):
                    eng.tensor_tensor(move_v[:, m, :], f_t[:, m, tok], coup[:, turn % 2, :], ALU.mult) \
                       .then_inc(s_mvv, 1)
                for m in range(EK):
                    wait(s_mvv, EK * number + m + 1)
                    wait(s_mvu, EK * turn + m + 1)
                    eng.tensor_tensor(v_t[:, m, tok], v_t[:, m, tok], move_v[:, m, :], ALU.subtract) \
                       .then_inc(s_vupd, 1)

            def coefficients(g):
                done = COEFS * g
                wait(s_ttok, g + 1)
                wait(s_gcs, g + 1)
                wait(s_tw, TT * GROUP * g)
                wait(s_fac, TT * GROUP * g)
                first = g * GROUP % XR

                def step(needs, out, *args, scalar=False):
                    nonlocal count
                    wait(s_coef, done + needs)
                    (eng.tensor_scalar if scalar else eng.tensor_tensor)(out, *args).then_inc(s_coef, 1)
                    count += 1

                count = 0
                by_batch = c_batch[:].unsqueeze(1).to_broadcast([P, CYCLES * TT, GROUP])
                all_c = tok_c[:].rearrange("p c (t b) -> p (c t) b", b=GROUP)
                deviation = rstd2[:, first:first + GROUP, :].rearrange("p b t -> p t b")
                minus_mean = neg_mean2[:, first:first + GROUP, :].rearrange("p b t -> p t b")

                def tb(buf):
                    return buf[:].rearrange("p (t b) -> p t b", b=GROUP)

                c1, c2, c3 = (tok_c[:, n, :] for n in range(CYCLES))
                step(0, tok_c[:].rearrange("p c a -> p (c a)"),
                     tok_th[:].rearrange("p c a -> p (c a)"), c_tok[:, 0:1], 1.0, ALU.mult, ALU.mult,
                     scalar=True)
                step(1, all_c, all_c, by_batch, ALU.add)
                step(2, c12[:], c1, c2, ALU.mult)
                step(2, co_b2[:], c1, c2, ALU.add)
                step(3, co_a2[:], c12[:], -1.0, 1.0, ALU.mult, ALU.add, scalar=True)
                step(4, c3b2[:], c3, co_b2[:], ALU.mult)
                step(5, c3a2[:], c3, co_a2[:], ALU.mult)
                step(6, co_a3[:], co_a2[:], c3b2[:], ALU.subtract)
                step(7, co_b3[:], co_b2[:], c3a2[:], ALU.add)
                step(8, tb(a3_r), tb(co_a3), deviation, ALU.mult)
                step(9, tb(b3_r), tb(co_b3), deviation, ALU.mult)
                step(10, x_fac[:], a3_r[:], 1.0, None, ALU.add, scalar=True)
                step(10, tb(x_add), tb(a3_r), minus_mean, ALU.mult)
                assert count == COEFS

            def factors(b):
                wait(s_coef, COEFS * (b // GROUP + 1))
                if b >= 2:
                    wait(s_res, 4 * (b - 1))
                for t in range(TT):
                    one = t * GROUP + b % GROUP
                    eng.tensor_scalar(twisted[:, b % 2, t, :], xy[:, b % XR, t * E:(t + 1) * E],
                                      neg_mean2[:, b % XR, t:t + 1], b3_r[:, one:one + 1],
                                      ALU.add, ALU.mult).then_inc(s_tw, 1)
                for t in range(TT):
                    one = t * GROUP + b % GROUP
                    wait(s_tw, TT * b + t + 1)
                    eng.tensor_scalar(xy[:, b % XR, t * E:(t + 1) * E], xy[:, b % XR, t * E:(t + 1) * E],
                                      x_fac[:, one:one + 1], x_add[:, one:one + 1],
                                      ALU.mult, ALU.add).then_inc(s_fac, 1)

            def low_half(g, chunk):
                number = CHUNKS * g + chunk
                wait(s_fhi, number + 1)
                tok, slot = slice(chunk * CT, (chunk + 1) * CT), number % 2
                eng.tensor_tensor(f_hl[:, slot, 1], f_t[:, :, tok], f_hl[:, slot, 0], ALU.subtract).then_inc(s_flo, 1)

            early, late = None, []
            for kind, i in slots():
                if kind == "ffn":
                    early = i * GROUP + GROUP + LAG
                    low_half(i, 1)
                    if early + 2 < NB:
                        prepare(early + 2)
                        query_hat(early + 2)
                        key_hat(early + 2)
                    low_half(i, 2)
                    low_half(i, 3)
                    for chunk in range(CHUNKS):
                        update_v(i, chunk)
                    late = list(range(i * GROUP, (i + 1) * GROUP))
                    continue
                if i >= LAG and (i - LAG + 1) % GROUP == 0:
                    low_half((i - LAG) // GROUP, 0)
                if i == early:
                    coefficients((i - LAG) // GROUP - 1)
                for b in late[:1]:
                    factors(b)
                late = late[1:]
                if i + 2 < NB and i != early:
                    prepare(i + 2)
                    query_hat(i + 2)
                    key_hat(i + 2)
                if 0 <= i - NORM_LAG < NB:
                    norm_2(i - NORM_LAG)
                if i + 2 < NB:
                    values(i + 2)
            coefficients(NGROUPS - 1)

        @block.vector
        def _(eng):
            wait = Waits(eng)
            wait(s_pool0, 4)
            eng.tensor_copy(ident16[:], ident[:]).then_inc(s_vec0, 1)
            wait(s_mask, 16)
            eng.tensor_copy(mask_f[:], mask_u8[:]).then_inc(s_vec0, 1)

            def attention_constants():
                wait(s_scal, 32)
                eng.tensor_scalar(u_scale[:], scal[:, 0:1], 1.0 / (Q_SCALE * K_SCALE * DH ** 0.5), None, ALU.mult) \
                   .then_inc(s_vec0, 1)
                wait(s_act0, 1)
                eng.tensor_scalar(shift[:], clip[:], -EXP_ROOM, 0.0, ALU.add, ALU.max).then_inc(s_vec0, 1)
                wait(s_pe0, 1)
                wait(s_vec0, 4)
                eng.tensor_scalar(exp_bias[:], banks(TR_BANK)[0:KEYS, 0:NB], MASKED, shift[0:KEYS, 0:1],
                                  ALU.mult, ALU.subtract).then_inc(s_vec0, 1)

            def weight_constants():
                wait(s_pool0, 8)
                wait(s_w, n_weights)
                eng.memset(w4rep[:], 0.0).then_inc(s_vec0, 1)
                eng.tensor_scalar(half_b4[:], scal[:, 2:3], 0.5, None, ALU.mult).then_inc(s_vec0, 1)
                eng.tensor_scalar(half_gb3[:], scal[:, 3:4], 0.5, None, ALU.mult).then_inc(s_vec0, 1)
                eng.tensor_scalar(neg_sign[:], sign[:], -1.0, None, ALU.mult).then_inc(s_vec0, 1)
                eng.tensor_reduce(w_max[:], w1, AX.XY, ALU.max, apply_absolute_value=True).then_inc(s_vec0, 1)
                eng.tensor_scalar(g3rep[0:G2, :], ones[0:G2, :], g3col[0:G2, 0:1], None, ALU.mult).then_inc(s_vec0, 1)
                wait(s_vec0, 6)
                eng.tensor_scalar(w4rep[0:M3, 0, :], ones[0:M3, :], w4col[0:M3, 0:1], None, ALU.mult).then_inc(s_vec0, 1)
                eng.tensor_scalar(w4rep[M3:P, 1, :], ones[M3:P, :], w4col[M3:P, 0:1], None, ALU.mult).then_inc(s_vec0, 1)
                eng.tensor_scalar(c_tok[:], scal[:, 4:5], 0.3, None, ALU.mult).then_inc(s_vec0, 1)
                eng.tensor_scalar(c_glob[:], scal[:, 4:5], 0.7, None, ALU.mult).then_inc(s_vec0, 1)
                wait(s_pe0, 2)
                eng.tensor_copy(wo_t[:].rearrange("p k e -> p (k e)"), banks(X_BANK)).then_inc(s_vec0, 1)

            def largest_weight():
                wait(s_pe0, 3)
                eng.tensor_reduce(w_row[:], banks(X_BANK)[0:1, 0:P], AX.X, ALU.max).then_inc(s_vec0, 1)

            def split_weights():
                wait(s_pe0, 4)
                eng.tensor_scalar(w_max[:], banks(X_BANK)[:, 0:1], TINY, None, ALU.max).then_inc(s_vec0, 1)
                wait(s_vec0, 18)
                eng.reciprocal(w_inv[:], w_max[:]).then_inc(s_vec0, 1)
                eng.tensor_scalar(uv_scale[:], w_max[:], 1.0 / (F_SCALE * W_SCALE), None, ALU.mult).then_inc(s_vec0, 1)
                wait(s_vec0, 19)
                eng.tensor_scalar(w1, w1, w_inv[:, 0:1], W_SCALE, ALU.mult, ALU.mult).then_inc(s_vec0, 1)
                wait(s_vec0, 21)
                eng.tensor_scalar(w1_twist[:, 1, :], w1[:, 0, :], sign[:, 0:1], None, ALU.mult).then_inc(s_vec0, 1)
                eng.tensor_scalar(w1_twist[:, 0, :], w1[:, 1, :], neg_sign[:, 0:1], None, ALU.mult) \
                   .then_inc(s_vec0, 1)
                eng.tensor_copy(w1_hl[:, 0], w1).then_inc(s_vec0, 1)
                wait(s_vec0, 23)
                eng.tensor_copy(w1t_hl[:, 0], w1_twist).then_inc(s_vec0, 1)
                wait(s_vec0, 25)
                eng.tensor_tensor(w1_hl[:, 1], w1, w1_hl[:, 0], ALU.subtract).then_inc(s_vec0, 1)
                eng.tensor_tensor(w1t_hl[:, 1], w1_twist, w1t_hl[:, 0], ALU.subtract).then_inc(s_vec0, 1)

            def stats(b):
                wait(s_ldx[b % NLOAD], 16 * (b // NLOAD + 1))
                for t in range(TT):
                    wait(s_mv, 2 * b)
                    eng.bn_stats(stats1[:, t, :], xy[:, b % XR, t * E:(t + 1) * E]).then_inc(s_stats, 1)
                if b >= 2:
                    wait(s_rstd, b - 1)
                    wait(s_mean, b - 1)
                for t in range(TT):
                    wait(s_stats, 2 * b + t + 1)
                    eng.bn_aggr(mv1[:, b % 2, t, :], stats1[:, t, :]).then_inc(s_mv, 1)

            def key_max(b):
                wait(s_ldc[b % NLOAD], 16 * (b // NLOAD + 1))
                wait(s_kamax, b)
                eng.tensor_reduce(k_max[:], cbuf[:, b % NLOAD, :], AX.X, ALU.max, apply_absolute_value=True) \
                   .then_inc(s_kmax, 1)

            def key_scale(b):
                wait(s_kmax, b + 1)
                wait(s_tsc, b)
                eng.tensor_scalar(k_amax[:], k_max[:], TINY, None, ALU.max).then_inc(s_kamax, 1)

            def key_inverse(b):
                wait(s_kamax, b + 1)
                wait(s_khat, b)
                eng.reciprocal(k_inv[:], k_amax[:]).then_inc(s_kinv, 1)
                if b >= 4:
                    wait(s_tanh, NG * (b - 3))
                eng.tensor_scalar(t_scale[:, b % 4, :], k_amax[:], u_scale[0:KEYS, 0:1], 1.0, ALU.mult, ALU.mult) \
                   .then_inc(s_tsc, 1)

            HEAD = 4 * 2 * DH

            def kz_heads(b, part):
                z = kz[:, b % 2, 0, part, 0, :]
                return bass.AP(z.tensor, z.offset, [list(z.ap[0]), [2 * HEAD, PAIRS], [HEAD + DH, 2], [1, DH]])

            def key_high(b):
                wait(s_khat, b + 1)
                wait(s_pool0, 8)
                if b >= 2:
                    wait(s_ktr, 2 * (b - 1))
                eng.tensor_copy(kz_heads(b, 0), k_hat[:].rearrange("k (p j d) -> k p j d", j=2, d=DH)) \
                   .then_inc(s_khi, 1)

            def key_low(b):
                wait(s_khi, b + 1)
                eng.tensor_tensor(kz_heads(b, 1), k_hat[:].rearrange("k (p j d) -> k p j d", j=2, d=DH),
                                  kz_heads(b, 0), ALU.subtract).then_inc(s_klo, 1)

            def key_twice(b):
                wait(s_klo, b + 1)
                eng.tensor_copy(kz[:, b % 2, :, :, 1, :], kz[:, b % 2, :, :, 0, :]).then_inc(s_kz, 1)

            q_pairs = q_hat[:].rearrange("p t (a d) -> p (t a) d", d=2 * DH)

            def q_part(b, part):
                return q_hl[:, b % 2].rearrange("p t a r h d -> p (t a) r h d")[:, :, 0, part, :]

            def query_high(b):
                wait(s_qhat, 2 * (b + 1))
                if b >= 2:
                    wait(s_qtr, 2 * (b - 1))
                eng.tensor_scalar(q_part(b, 0), q_pairs, Q_SCALE, None, ALU.mult).then_inc(s_qhi, 1)

            def query_low(b):
                wait(s_qhi, b + 1)
                eng.scalar_tensor_tensor(q_part(b, 1), q_pairs, Q_SCALE, q_part(b, 0),
                                         ALU.mult, ALU.subtract).then_inc(s_qlo, 1)

            def query_twice(b):
                wait(s_qlo, b + 1)
                both = q_hl[:, b % 2].rearrange("p t a r h d -> p (t a) r (h d)")
                eng.tensor_copy(both[:, :, 1, :], both[:, :, 0, :]).then_inc(s_qhl, 1)

            def q_stack(b, t):
                wait(s_qtr, 2 * b + t + 1)
                if b >= 2:
                    wait(s_score, NG * (b - 1))
                eng.tensor_copy(q_st[:, b % 2, :, t * P:(t + 1) * P],
                                banks(TR_BANK).bitcast(F16).rearrange("p (a q) -> p a q", q=P)).then_inc(s_qst, 1)

            def k_stack(b, n):
                wait(s_ktr, 2 * b + n + 1)
                if b >= 2:
                    wait(s_score, NG * (b - 1))
                eng.tensor_copy(k_st[:, b % 2, n * PAIRS:(n + 1) * PAIRS, :],
                                banks(TR_BANK).bitcast(F16)[:, 0:PAIRS * KEYS].rearrange("p (a q) -> p a q", q=KEYS)) \
                   .then_inc(s_kst, 1)

            def divide(b):
                for t in range(TT):
                    heads = banks(PV_BANKS[t]).rearrange("p (h s) -> p h s", s=SLOT)
                    wait(s_otr, 2 * b + t + 1)
                    wait(s_otok, 2 * (b - 1) + t + 1)
                    eng.reciprocal(inv_sum[:, t, :], heads[:, :, DH]).then_inc(s_inv, 1)
                for t in range(TT):
                    heads = banks(PV_BANKS[t]).rearrange("p (h s) -> p h s", s=SLOT)
                    wait(s_inv, 2 * b + t + 1)
                    wait(s_oftr, b)
                    eng.tensor_tensor(o_tok[:, t, :].rearrange("p (h d) -> p h d", d=DH), heads[:, :, 0:DH],
                                      inv_sum[:, t, :].unsqueeze(2).to_broadcast([P, H, DH]), ALU.mult) \
                       .then_inc(s_otok, 1)

            def attn_features(b):
                wait(s_oftr, b + 1)
                wait(s_proj, b)
                eng.tensor_copy(of_t[:].rearrange("p k q -> p (k q)"), banks(X_BANK)).then_inc(s_oft, 1)

            def residual(b):
                wait(s_proj, b + 1)
                eng.tensor_tensor(xy[:, b % XR, :], xy[:, b % XR, :], banks(X_BANK), ALU.add).then_inc(s_y, 1)

            def stats_2(b):
                wait(s_y, b + 1)
                wait(s_mv2, 2 * b)
                for t in range(TT):
                    eng.bn_stats(stats2[:, t, :], xy[:, b % XR, t * E:(t + 1) * E]).then_inc(s_stats2, 1)
                wait(s_rstd2, b)
                wait(s_mean2, b)
                for t in range(TT):
                    wait(s_stats2, 2 * b + t + 1)
                    eng.bn_aggr(mv2[:, t, :], stats2[:, t, :]).then_inc(s_mv2, 1)

            def high_half(g, chunk):
                number = CHUNKS * g + chunk
                wait(s_ft, 2 * (g * GROUP + (chunk + 1) * CB))
                if number >= 2:
                    wait(s_l1, 2 * EK * (number - 1))
                eng.tensor_copy(f_hl[:, number % 2, 0], f_t[:, :, chunk * CT:(chunk + 1) * CT]).then_inc(s_fhi, 1)

            def first_layer_out(g, chunk):
                number = CHUNKS * g + chunk
                tok = slice(chunk * CT, (chunk + 1) * CT)
                wait(s_flo, number + 1)
                if g:
                    wait(s_upd, EK * (UPDATES * (g - 1) + CHUNKS + chunk + 1))
                for m in range(EK):
                    wait(s_l1, 2 * EK * number + m + 1)
                    eng.tensor_scalar(v_t[:, m, tok], banks(V_BANKS[m]), uv_scale[:, 0:1], None, ALU.mult) \
                       .then_inc(s_uv, 1)
                wait(s_l1, 2 * EK * (number + 1))
                for m in range(EK):
                    wait(s_h1, EK * (PASSES * g + chunk) + m + 1)
                    eng.tensor_scalar(f_t[:, m, tok], banks(U_BANKS[m]), uv_scale[:, 0:1], None, ALU.mult) \
                       .then_inc(s_uv, 1)

            def couple(g, p):
                turn, chunk = UPDATES * g + p, slot_of(p)[1]
                wait(s_th, turn + 1)
                wait(s_gcs, g + 1)
                for b in range(CB):
                    c = coup[:, turn % 2, b * S:(b + 1) * S]
                    eng.tensor_scalar(c, c, c_tok[:, 0:1], c_batch[:, chunk * CB + b:chunk * CB + b + 1],
                                      ALU.mult, ALU.add).then_inc(s_coup, 1)

            def update_u(g, p):
                cyc, chunk = slot_of(p)
                turn, number = UPDATES * g + p, CHUNKS * g + chunk
                tok = slice(chunk * CT, (chunk + 1) * CT)
                wait(s_coup, CB * (turn + 1))
                if cyc == 0:
                    wait(s_uv, 2 * EK * (number + 1))
                else:
                    wait(s_vupd, EK * (number + 1))
                    wait(s_h1, EK * (PASSES * g + p + 1))
                wait(s_upd, EK * turn)
                for m in range(EK):
                    eng.tensor_tensor(move_u[:, m, :], v_t[:, m, tok], coup[:, turn % 2, :], ALU.mult) \
                       .then_inc(s_mvu, 1)
                for m in range(EK):
                    wait(s_mvu, EK * turn + m + 1)
                    if cyc == 0:
                        wait(s_mvv, EK * number + m + 1)
                    eng.tensor_tensor(f_t[:, m, tok], f_t[:, m, tok], move_u[:, m, :], ALU.add).then_inc(s_upd, 1)

            def twist_source(b):
                wait(s_tw, TT * b)
                wait(s_coef, COEFS * NGROUPS)
                wait(s_res, 4 * (b - 1))
                for t in range(TT):
                    one = t * GROUP + b % GROUP
                    eng.tensor_scalar(twisted[:, b % 2, t, :], xy[:, b % XR, t * E:(t + 1) * E],
                                      neg_mean2[:, b % XR, t:t + 1], b3_r[:, one:one + 1],
                                      ALU.add, ALU.mult).then_inc(s_tw, 1)

            def combine(b):
                wait(s_fac, TT * (b + 1))
                wait(s_tw, TT * (b + 1))
                q = E // 4
                y = xy[:, b % XR, :].rearrange("p (t e) -> p t e", t=TT)
                for part, (source, op) in enumerate(((2, ALU.add), (3, ALU.subtract), (0, ALU.subtract), (1, ALU.add))):
                    at = y[:, :, part * q:(part + 1) * q]
                    eng.tensor_tensor(at, at, twisted[:, b % 2, :, source * q:(source + 1) * q], op).then_inc(s_res, 1)

            def second_norm(b):
                residual(b)
                stats_2(b)

            late, early = [], None
            for kind, i in slots():
                if i == 2 and kind == "attention":
                    split_weights()
                if kind == "attention":
                    new, nxt, old, last = i + 2, i + 1, i - 2, i - NORM_LAG
                    fresh, ahead, past = new < NB and i != early, 0 <= nxt < NB, 0 <= old < NB
                    if 0 <= last < NB and i != early:
                        second_norm(last)
                    if i >= LAG and (i - LAG + 1) % GROUP == 0:
                        high_half((i - LAG) // GROUP, 0)
                    if ahead:
                        q_stack(nxt, 0)
                    if past:
                        divide(old)
                    if fresh:
                        stats(new)
                        key_max(new)
                    if i == -2:
                        attention_constants()
                    if ahead:
                        q_stack(nxt, 1)
                    if fresh:
                        key_scale(new)
                    for b in late[:1]:
                        combine(b)
                    late = late[1:]
                    if fresh:
                        key_inverse(new)
                    if ahead:
                        k_stack(nxt, 0)
                    if past:
                        attn_features(old)
                    if fresh:
                        query_high(new)
                        key_high(new)
                    if ahead:
                        k_stack(nxt, 1)
                    if fresh:
                        query_low(new)
                        key_low(new)
                        query_twice(new)
                        key_twice(new)
                    if i == 0:
                        weight_constants()
                    if i == 1:
                        largest_weight()
                else:
                    early = i * GROUP + GROUP + LAG
                    new = early + 2
                    high_half(i, 1)
                    if early - NORM_LAG < NB:
                        second_norm(early - NORM_LAG)
                    if new < NB:
                        stats(new)
                        key_max(new)
                        key_scale(new)
                        key_inverse(new)
                    first_layer_out(i, 0)
                    high_half(i, 2)
                    first_layer_out(i, 1)
                    high_half(i, 3)
                    first_layer_out(i, 2)
                    for p in range(PASSES):
                        if p == 0:
                            wait(s_gact, 3 * (i + 1))
                            wait(s_coef, COEFS * i)
                            eng.tensor_scalar(c_batch[:], gth[:], c_glob[:, 0:1], 0.1, ALU.mult, ALU.add) \
                               .then_inc(s_gcs, 1)
                        if p < UPDATES:
                            couple(i, p)
                            update_u(i, p)
                        if p == 0:
                            first_layer_out(i, 3)
                    if new < NB:
                        query_high(new)
                        key_high(new)
                        query_low(new)
                        key_low(new)
                        query_twice(new)
                        key_twice(new)
                    late = list(range(i * GROUP, (i + 1) * GROUP))
            for b in late:
                twist_source(b)
                combine(b)

        @block.scalar
        def _(eng):
            wait = Waits(eng)
            wait(s_scal, 32)
            eng.activation(clip[:], scal[:, 1:2], ACT.Exp).then_inc(s_act0, 1)

            def tanh(b, n):
                wait(s_score, NG * b + n + 1)
                wait(s_tsc, b + 1)
                if b >= 2:
                    wait(s_pv, 2 * (b - 2) + n // 2 + 1)
                first = SCORE_BANKS[n % 2][0]
                eng.activation(probs[:, b % 2, n * HG:(n + 1) * HG, :].rearrange("k h q -> k (h q)"),
                               banks(first, 2)[0:KEYS, :], ACT.Tanh, scale=t_scale[:, b % 4, :]).then_inc(s_tanh, 1)

            def exp(b, n):
                wait(s_tanh, NG * b + 2 * n + 2)
                p = probs[:, b % 2, 2 * n * HG:2 * (n + 1) * HG, :].rearrange("k h q -> k (h q)")
                eng.activation(p, p, ACT.Exp, scale=clip[0:KEYS, 0:1], bias=exp_bias[:, b:b + 1]).then_inc(s_exp, 1)

            def attn_out(b, n):
                wait(s_pv, 2 * b + n + 1)
                if b >= 2:
                    wait(s_otr, 2 * (b - 1))
                eng.activation(o_t[:, b % 2, 2 * n:2 * n + 2, :].rearrange("p c q -> p (c q)"),
                               banks(PV_BANKS[n]), ACT.Copy).then_inc(s_ot, 1)

            def features(b):
                wait(s_ftr, b + 1)
                if b >= GROUP:
                    g, chunk = b // GROUP, b % GROUP // CB
                    wait(s_h1, EK * (PASSES * (g - 1) + (CYCLES - 1) * CHUNKS + chunk + 1))
                    wait(s_glob, 3 * g)
                at = b % GROUP
                for k in range(EK):
                    eng.activation(f_t[:, k, at * S:(at + 1) * S], banks(X_BANK)[:, k * S:(k + 1) * S],
                                   ACT.Identity, scale=F_SCALE, accum_out=f_sum[:, k, at:at + 1]).then_inc(s_ft, 1)

            def gelu1(g, p):
                (cyc, chunk), n = slot_of(p), PASSES * g + p
                if n >= 2:
                    wait(s_l2, n - 1)
                for m in range(EK):
                    if cyc == 0:
                        wait(s_w, n_weights)
                        wait(s_vec0, N_SPLIT)
                        wait(s_l1, 2 * EK * (CHUNKS * g + chunk) + EK + m + 1)
                        source, by = banks(U_BANKS[m]), uv_scale[:, 0:1]
                    else:
                        wait(s_upd, EK * (UPDATES * g + p - CHUNKS) + m + 1)
                        source, by = f_t[:, m, chunk * CT:(chunk + 1) * CT], 1.0
                    eng.activation(h1[:, p % 2, m, :], source, ACT.Gelu, bias=b1[:, m:m + 1], scale=by) \
                       .then_inc(s_h1, 1)

            def gelu2(g, p):
                n = PASSES * g + p
                wait(s_l2, n + 1)
                if n >= 2:
                    wait(s_l3, n - 1)
                eng.activation(h2[:, p % 2, :], banks(L2_BANKS[p % 2]), ACT.Gelu, bias=b2[:, 0:1]).then_inc(s_h2, 1)

            def gelu3(g, p):
                n = PASSES * g + p
                wait(s_l3, n + 1)
                if n >= 2:
                    wait(s_ztok, n - 1)
                eng.activation(h3[:, p % 2, :], banks(L3_BANK)[:, 0:S], ACT.Gelu, bias=b3[:, 0:1]).then_inc(s_h3, 1)

            def tanh4(g, p):
                turn = UPDATES * g + p
                wait(s_l4, turn + 1)
                if turn >= 2:
                    wait(s_mvu, EK * (turn - 1))
                    before, cyc_before = (turn - 2) // UPDATES, (turn - 2) % UPDATES // CHUNKS
                    if cyc_before == 0:
                        wait(s_mvv, EK * (CHUNKS * before + (turn - 2) % UPDATES + 1))
                eng.activation(coup[:, turn % 2, :], banks(L4_BANK), ACT.Tanh, scale=0.5,
                               bias=half_b4[:, 0:1]).then_inc(s_th, 1)

            def token_tanh(g):
                wait(s_ztok, PASSES * (g + 1))
                wait(s_coef, COEFS * g)
                eng.activation(tok_th[:].rearrange("p c a -> p (c a)"),
                               banks(TR_BANK)[:, TOKEN_AT:TOKEN_AT + CYCLES * GT], ACT.Tanh, scale=0.5,
                               bias=half_b4[:, 0:1]).then_inc(s_ttok, 1)

            def x_part(b):
                wait(s_coef, COEFS * NGROUPS)
                wait(s_tw, TT * (b + 1))
                wait(s_fac, TT * b)
                for t in range(TT):
                    one = t * GROUP + b % GROUP
                    here = xy[:, b % XR, t * E:(t + 1) * E]
                    eng.activation(here, here, ACT.Identity, scale=x_fac[:, one:one + 1],
                                   bias=x_add[:, one:one + 1]).then_inc(s_fac, 1)

            wait(s_vec0, N_BIAS)
            for kind, i in slots():
                if kind == "attention":
                    on, past = 0 <= i < NB, 0 <= i - 1 < NB
                    if on:
                        tanh(i, 0)
                        tanh(i, 1)
                        exp(i, 0)
                    if 0 <= i - LAG < NB:
                        features(i - LAG)
                    if past:
                        attn_out(i - 1, 1)
                    if on:
                        tanh(i, 2)
                        tanh(i, 3)
                        exp(i, 1)
                        attn_out(i, 0)
                else:
                    glob = banks(TR_BANK)[:, SMALL_AT:SMALL_AT + 3 * GROUP]
                    gelu1(i, 0)
                    for p in range(PASSES + 2):
                        if p == 0:
                            wait(s_glob, 3 * i + 1)
                            eng.activation(gh1[:], glob[:, 0:GROUP], ACT.Gelu, bias=gb1[:, 0:1],
                                           scale=1.0 / (S * F_SCALE)) \
                               .then_inc(s_gact, 1)
                        if 0 <= p - 2 < UPDATES:
                            tanh4(i, p - 2)
                        if p == 1:
                            wait(s_glob, 3 * i + 3)
                            wait(s_gcs, i)
                            eng.activation(gth[:], glob[:, 2 * GROUP:3 * GROUP], ACT.Tanh, scale=0.5,
                                           bias=half_gb3[:, 0:1]).then_inc(s_gact, 1)
                            gelu1(i, p + 1)
                        last_cycle = UPDATES < p < PASSES
                        if last_cycle:
                            if p + 1 < PASSES:
                                gelu1(i, p + 1)
                            gelu2(i, p)
                        if 0 <= p - 1 < PASSES:
                            gelu3(i, p - 1)
                        if p + 1 < CHUNKS and p != 1:
                            gelu1(i, p + 1)
                        if p == 0:
                            wait(s_glob, 3 * i + 2)
                            eng.activation(gh2[0:G2, :], glob[0:G2, GROUP:2 * GROUP], ACT.Gelu, bias=gb2[0:G2, 0:1]) \
                               .then_inc(s_gact, 1)
                        if p < PASSES and not last_cycle:
                            gelu2(i, p)
                        if CHUNKS <= p + 1 < PASSES and not last_cycle:
                            gelu1(i, p + 1)
                    token_tanh(i)
            for b in range(NB - GROUP, NB):
                x_part(b)

        @block.tensor
        def _(eng):
            wait = Waits(eng)
            reader = {}

            def claim(*which):
                for bank in which:
                    for step in reader.get(bank, ()):
                        wait(*step)

            def read_by(s, n, *which):
                for bank in which:
                    reader[bank] = [(s, n)]

            wait(s_pool0, 3)
            wait(s_vec0, N_MASK)
            eng.transpose(banks(TR_BANK)[0:KEYS, 0:NB], mask_f[:], ident[0:NB, 0:NB]).then_inc(s_pe0, 1)
            read_by(s_vec0, N_BIAS, TR_BANK)

            def transpose_w_out():
                wait(s_w, n_weights)
                for k in range(EK):
                    for m in range(EK):
                        last = eng.transpose(banks(X_BANK)[:, k * E + m * P:k * E + (m + 1) * P],
                                             wo_in[:, m, k * P:(k + 1) * P], ident[:])
                last.then_inc(s_pe0, 1)
                read_by(s_vec0, N_WO, X_BANK)

            def largest_beside():
                wait(s_vec0, N_MAX)
                claim(X_BANK)
                eng.transpose(banks(X_BANK)[0:1, 0:P], w_max[:], ident[:]).then_inc(s_pe0, 1)
                read_by(s_vec0, N_ROW, X_BANK)

            def largest_spread():
                wait(s_pool0, 8)
                claim(X_BANK)
                eng.matmul(banks(X_BANK)[:, 0:1], ones[0:1, :], w_row[:], start=True, stop=True).then_inc(s_pe0, 1)
                read_by(s_vec0, N_SPREAD, X_BANK)

            def query_stack(b, t):
                wait(s_qhl, b + 1)
                claim(TR_BANK)
                dst = banks(TR_BANK).bitcast(F16)
                for pair in range(PAIRS):
                    last = eng.transpose(dst[:, pair * P:(pair + 1) * P],
                                         q_hl[:, b % 2, t, pair].rearrange("p r h d -> p (r h d)"), ident16[:])
                last.then_inc(s_qtr, 1)
                read_by(s_qst, 2 * b + t + 1, TR_BANK)

            def key_stack(b, n):
                wait(s_kz, b + 1)
                claim(TR_BANK)
                dst = banks(TR_BANK).bitcast(F16)
                for j in range(PAIRS):
                    last = eng.transpose(dst[:, j * KEYS:(j + 1) * KEYS],
                                         kz[:, b % 2, n * PAIRS + j].rearrange("k h r d -> k (h r d)"),
                                         ident16[0:KEYS, 0:KEYS])
                last.then_inc(s_ktr, 1)
                read_by(s_kst, 2 * b + n + 1, TR_BANK)

            def scores(b, n):
                wait(s_qst, 2 * (b + 1))
                wait(s_kst, 2 * b + n // 2 + 1)
                pair_of_banks = SCORE_BANKS[n % 2]
                claim(*pair_of_banks)
                for j in range(HG):
                    h = n * HG + j
                    last = eng.matmul(banks(pair_of_banks[0], 2)[0:KEYS, j * S:(j + 1) * S],
                                      k_st[:, b % 2, h, :], q_st[:, b % 2, h // 2, :], start=True, stop=True)
                last.then_inc(s_score, 1)
                read_by(s_tanh, NG * b + n + 1, *pair_of_banks)

            def weighted_values(b, n):
                wait(s_exp, 2 * b + n + 1)
                wait(s_va, b + 1)
                claim(PV_BANKS[n])
                for c in (2 * n, 2 * n + 1):
                    for j in range(HG):
                        h = c * HG + j
                        last = eng.matmul(banks(PV_BANKS[n])[j * SLOT:(j + 1) * SLOT, (c % 2) * S:(c % 2 + 1) * S],
                                          va[:, b % 3, h, :], probs[:, b % 2, h, :], start=True, stop=True,
                                          tile_position=(0, j * SLOT))
                last.then_inc(s_pv, 1)
                read_by(s_ot, 2 * b + n + 1, PV_BANKS[n])

            def attn_to_tokens(b):
                wait(s_ot, 2 * (b + 1))
                for t in range(TT):
                    claim(PV_BANKS[t])
                    for c in range(NG):
                        last = eng.transpose(banks(PV_BANKS[t])[:, c * P:(c + 1) * P],
                                             o_t[:, b % 2, c, t * P:(t + 1) * P], ident[:])
                    last.then_inc(s_otr, 1)
                    read_by(s_otok, 2 * b + t + 1, PV_BANKS[t])

            def attn_to_features(b):
                wait(s_otok, 2 * (b + 1))
                claim(X_BANK)
                for k in range(EK):
                    for t in range(TT):
                        last = eng.transpose(banks(X_BANK)[:, k * S + t * P:k * S + (t + 1) * P],
                                             o_tok[:, t, k * P:(k + 1) * P], ident[:])
                last.then_inc(s_oftr, 1)
                read_by(s_oft, b + 1, X_BANK)

            def project(b):
                wait(s_oft, b + 1)
                claim(X_BANK)
                for t in range(TT):
                    for k in range(EK):
                        last = eng.matmul(banks(X_BANK)[:, t * E:(t + 1) * E], of_t[:, k, t * P:(t + 1) * P],
                                          wo_t[:, k, :], start=(k == 0), stop=(k == EK - 1))
                last.then_inc(s_proj, 1)
                read_by(s_y, b + 1, X_BANK)

            def norm_to_features(b):
                wait(s_fhat, 2 * (b + 1))
                claim(X_BANK)
                for k in range(EK):
                    for t in range(TT):
                        last = eng.transpose(banks(X_BANK)[:, k * S + t * P:k * S + (t + 1) * P],
                                             f_hat[:, t, k * P:(k + 1) * P], ident[:])
                last.then_inc(s_ftr, 1)
                read_by(s_ft, 2 * (b + 1), X_BANK)

            def layer1(g, chunk):
                number = CHUNKS * g + chunk
                wait(s_vec0, N_SPLIT)
                wait(s_flo, number + 1)
                halves = f_hl[:, number % 2]
                products = [(w, f, k) for w, f in ((0, 0), (0, 1), (1, 0)) for k in range(EK)]
                for weights, where in ((w1t_hl, V_BANKS), (w1_hl, U_BANKS)):
                    for m in range(EK):
                        claim(where[m])
                        for n, (w, f, k) in enumerate(products):
                            last = eng.matmul(banks(where[m]), weights[:, w, k, m * P:(m + 1) * P], halves[:, f, k, :],
                                              start=(n == 0), stop=(n == len(products) - 1))
                        last.then_inc(s_l1, 1)
                for m in range(EK):
                    reader[V_BANKS[m]] = [(s_uv, 2 * EK * number + m + 1)]
                    reader[U_BANKS[m]] = [(s_uv, 2 * EK * number + EK + m + 1)]

            def layer2(g, p):
                n = PASSES * g + p
                bank = L2_BANKS[p % 2]
                claim(bank)
                for k in range(EK):
                    wait(s_h1, EK * n + k + 1)
                    last = eng.matmul(banks(bank), w2[:, k, :], h1[:, p % 2, k, :], start=(k == 0), stop=(k == EK - 1))
                last.then_inc(s_l2, 1)
                read_by(s_h2, n + 1, bank)

            def layer3(g, p):
                n = PASSES * g + p
                wait(s_h2, n + 1)
                wait(s_h3, n)
                wait(s_gact, 3 * (g + 1))
                for b in range(CB):
                    last = eng.matmul(banks(L3_BANK)[b * M3:(b + 1) * M3, 0:S], w3[:],
                                      h2[:, p % 2, b * S:(b + 1) * S], start=True, stop=True,
                                      tile_position=(0, b * M3))
                last.then_inc(s_l3, 1)

            def layer4(g, p):
                turn = UPDATES * g + p
                wait(s_h3, PASSES * g + p + 1)
                claim(L4_BANK)
                for b in range(CB):
                    last = eng.matmul(banks(L4_BANK)[:, b * S:(b + 1) * S], w4rep[:, b, :], h3[:, p % 2, :],
                                      start=True, stop=True)
                last.then_inc(s_l4, 1)
                read_by(s_th, turn + 1, L4_BANK)

            def token_output(g, p):
                (cyc, chunk), n = slot_of(p), PASSES * g + p
                wait(s_h3, n + 1)
                for t in range(TT):
                    at = TOKEN_AT + (cyc * TT + t) * GROUP + chunk * CB
                    last = eng.matmul(banks(TR_BANK)[:, at:at + CB], h3[:, p % 2, t * P:(t + 1) * P],
                                      w4rep[:, :, 0], start=True, stop=True)
                last.then_inc(s_ztok, 1)

            def global_net(g, layer):
                dst = banks(TR_BANK)[:, SMALL_AT:SMALL_AT + 3 * GROUP]
                if layer == 0:
                    wait(s_ft, 2 * (g + 1) * GROUP)
                    claim(TR_BANK)
                    for k in range(EK):
                        last = eng.matmul(dst[:, 0:GROUP], g1[:, k, :], f_sum[:, k, :], start=(k == 0), stop=(k == EK - 1))
                else:
                    wait(s_gact, 3 * g + layer)
                    if layer == 1:
                        last = eng.matmul(dst[0:G2, GROUP:2 * GROUP], g2[:], gh1[:], start=True, stop=True)
                    else:
                        last = eng.matmul(dst[:, 2 * GROUP:3 * GROUP], g3rep[0:G2, :], gh2[0:G2, :],
                                          start=True, stop=True)
                last.then_inc(s_glob, 1)

            early = None
            for kind, i in slots():
                if kind == "attention":
                    nxt, done, old = i + 1, i - 1, i - 2
                    on, ahead, past, older = 0 <= i < NB, 0 <= nxt < NB, 0 <= done < NB, 0 <= old < NB
                    if i == 2:
                        largest_spread()
                    if on and i != early:
                        scores(i, 0)
                        scores(i, 1)
                    if ahead:
                        query_stack(nxt, 0)
                    if 0 <= i - LAG < NB:
                        norm_to_features(i - LAG)
                    if older:
                        attn_to_tokens(old)
                    if ahead:
                        query_stack(nxt, 1)
                    if past:
                        weighted_values(done, 1)
                    if on:
                        scores(i, 2)
                        scores(i, 3)
                    if ahead:
                        key_stack(nxt, 0)
                    if older:
                        attn_to_features(old)
                    if on:
                        weighted_values(i, 0)
                    if ahead:
                        key_stack(nxt, 1)
                    if older:
                        project(old)
                    if i == 0:
                        transpose_w_out()
                    if i == 1:
                        largest_beside()
                else:
                    early = i * GROUP + GROUP + LAG
                    layer1(i, 0)
                    for p in range(PASSES + 2):
                        if p == 0:
                            global_net(i, 0)
                        if p == 1:
                            global_net(i, 2)
                        if p == PASSES and early < NB:
                            scores(early, 0)
                        if 0 <= p - 2 < UPDATES:
                            layer4(i, p - 2)
                        last_cycle = UPDATES < p < PASSES
                        if last_cycle:
                            layer2(i, p)
                        if p >= 2:
                            token_output(i, p - 2)
                        if p == 1:
                            layer1(i, p + 1)
                        if 0 <= p - 1 < PASSES:
                            layer3(i, p - 1)
                        if p == PASSES and early < NB:
                            scores(early, 1)
                        if p + 1 < CHUNKS and p != 1:
                            layer1(i, p + 1)
                        if p == 0:
                            global_net(i, 1)
                        if p < PASSES and not last_cycle:
                            layer2(i, p)
                    read_by(s_ttok, i + 1, TR_BANK)


_INS = ['x', 'ctx_1024', 'mask_Bx1xS2_bk0', 'L0_xattn_W_out', 'L0_xattn_scale', 'L0_xattn_log_C',
        'L0_ffn_cn_w1', 'L0_ffn_cn_b1', 'L0_ffn_cn_w2', 'L0_ffn_cn_b2', 'L0_ffn_cn_w3', 'L0_ffn_cn_b3',
        'L0_ffn_cn_w4', 'L0_ffn_cn_b4', 'L0_ffn_gc_w1', 'L0_ffn_gc_b1', 'L0_ffn_gc_w2', 'L0_ffn_gc_b2',
        'L0_ffn_gc_w3', 'L0_ffn_gc_b3', 'L0_ffn_adaptive_range']


def kernel(**inputs):
    import numpy as _np
    import concourse.bacc as _bacc
    from concourse import mybir as _mybir
    from concourse.bass_utils import run_bass_kernel_spmd as _run

    nc = _bacc.Bacc("TRN2", target_bir_lowering=False, num_devices=1)
    arrays, args = {}, []
    for name in _INS:
        a = _np.ascontiguousarray(inputs[name])
        a = a.reshape(a.shape or (1,))
        arrays[f"in_{name}_dram"] = a
        args.append(nc.dram_tensor(f"in_{name}_dram", a.shape, _mybir.dt.from_np(a.dtype), kind="ExternalInput").ap())
    shape = tuple(inputs['x'].shape)
    args.append(nc.dram_tensor("out_0_dram", shape, _mybir.dt.float32, kind="ExternalOutput").ap())
    xattn_ffn_kernel(nc, *args)
    r = _run(nc, [arrays], core_ids=[0])
    return r.results[0]["out_0_dram"]
```
